# Optimizing a Trainium2 kernel written in Bass

```python
import numpy as np
import jax
import jax.numpy as jnp

def _softmax(x, axis=-1):
    return jax.nn.softmax(x, axis=axis)

def _gelu(x):
    return jax.nn.gelu(x, approximate=True)

def _silu(x):
    return jax.nn.silu(x)

def _sigmoid(x):
    return jax.nn.sigmoid(x)

def _layernorm(x, axis=-1, eps=1e-05):
    m = jnp.mean(x, axis=axis, keepdims=True)
    v = jnp.var(x, axis=axis, keepdims=True)
    return (x - m) / jnp.sqrt(v + eps)

def _scatter_add(tgt, idx, src, axis=0):
    return tgt.at[idx].add(src)

def _segment_sum(src, seg, n):
    return jax.ops.segment_sum(src, seg, n)
kernel_name = 'mk_xattn_ffn_d1_seqx_r4_cb5258'

def setup_inputs(seed: int=0):
    np.random.seed(seed)
    _w = jnp.asarray

    def _rec_inputs():
        import jax
        import jax.numpy as jnp
        _rk = jax.random.key(seed)
        x = 7.22e-05 + 1 * jax.random.normal(jax.random.fold_in(_rk, 1), (64, 128, 256), jnp.float32)
        _lenS = 128 - jax.random.randint(jax.random.fold_in(_rk, 7), (64,), 0, max(1, 128 // 4) + 1, jnp.int32)
        _lenS2 = 128 - jax.random.randint(jax.random.fold_in(_rk, 8), (64,), 0, max(1, 128 // 4) + 1, jnp.int32)
        _ctx_1024P = jax.random.normal(jax.random.fold_in(_rk, 11), (64, 16, 256), jnp.float32)
        _ctx_1024c = jax.random.dirichlet(jax.random.fold_in(_rk, 511), 0.3 * jnp.ones((16,), jnp.float32), (64, 128))
        _ctx_1024t = jnp.einsum('bsk,bkd->bsd', _ctx_1024c, _ctx_1024P)
        _ctx_1024t = _ctx_1024t * jax.lax.rsqrt(jnp.mean(jnp.square(_ctx_1024t)) + 1e-12) * 0.953939
        ctx_1024 = 4.13588e-05 + 0.999923 * (_ctx_1024t + 0.3 * jax.random.normal(jax.random.fold_in(_rk, 611), (64, 128, 256), jnp.float32))
        return (x, ctx_1024)
    x, ctx_1024 = _rec_inputs()

    def _L0_xattn_setup():
        import jax, jax.numpy as jnp
        import numpy as np
        import math
        B, S, D, H = (4, 512, 256, 16)
        DH = D // H

        def _split_heads(x):
            b, s, _ = x.shape
            return x.reshape(b, s, H, DH).transpose(0, 2, 1, 3)
        key = jax.random.key(seed)
        ks = jax.random.split(key, 12)
        sc = 1.0 / math.sqrt(D)
        return {'x_q': jax.random.normal(ks[0], (B, S, D), jnp.float32), 'x_kv': jax.random.normal(ks[1], (B, S, D), jnp.float32), 'W_q': jax.random.normal(ks[2], (D, D), jnp.float32) * sc, 'b_q': jnp.zeros((D,), jnp.float32), 'W_k': jax.random.normal(ks[3], (D, D), jnp.float32) * sc, 'b_k': jnp.zeros((D,), jnp.float32), 'W_v': jax.random.normal(ks[4], (D, D), jnp.float32) * sc, 'b_v': jnp.zeros((D,), jnp.float32), 'W_out': jax.random.normal(ks[5], (D, D), jnp.float32) * sc, 'b_out': jnp.zeros((D,), jnp.float32)}
    _L0_xattn_all = _L0_xattn_setup()
    _L0_xattn_in = {k: v for k, v in _L0_xattn_all.items() if k in ('W_q', 'b_q', 'W_k', 'b_k', 'W_v', 'b_v', 'W_out', 'b_out')}
    del _L0_xattn_all

    def _L0_ffn_setup():
        import jax, jax.numpy as jnp
        import numpy as np
        D = 256
        H = 512
        E = 8
        K = 2
        B, T = (4, 512)
        key = jax.random.key(seed)
        ks = jax.random.split(key, 7)
        s = 0.02
        return {'x': jax.random.normal(ks[0], (B, T, D), dtype=jnp.float32), 'W1': jax.random.normal(ks[1], (E, D, 2 * H), dtype=jnp.float32) * s, 'b1': jnp.zeros((E, 2 * H), dtype=jnp.float32), 'W2': jax.random.normal(ks[2], (E, H, D), dtype=jnp.float32) * s, 'b2': jnp.zeros((E, D), dtype=jnp.float32), 'Wr': jax.random.normal(ks[3], (D, E), dtype=jnp.float32) * s, 'br': jnp.zeros((E,), dtype=jnp.float32)}
    _L0_ffn_all = _L0_ffn_setup()
    _L0_ffn_in = {k: v for k, v in _L0_ffn_all.items() if k in ('W1', 'b1', 'W2', 'b2', 'Wr', 'br')}
    del _L0_ffn_all
    return {'x': x, 'ctx_1024': ctx_1024, 'L0_xattn_W_q': _L0_xattn_in['W_q'], 'L0_xattn_b_q': _L0_xattn_in['b_q'], 'L0_xattn_W_k': _L0_xattn_in['W_k'], 'L0_xattn_b_k': _L0_xattn_in['b_k'], 'L0_xattn_W_v': _L0_xattn_in['W_v'], 'L0_xattn_b_v': _L0_xattn_in['b_v'], 'L0_xattn_W_out': _L0_xattn_in['W_out'], 'L0_xattn_b_out': _L0_xattn_in['b_out'], 'L0_ffn_W1': _L0_ffn_in['W1'], 'L0_ffn_b1': _L0_ffn_in['b1'], 'L0_ffn_W2': _L0_ffn_in['W2'], 'L0_ffn_b2': _L0_ffn_in['b2'], 'L0_ffn_Wr': _L0_ffn_in['Wr'], 'L0_ffn_br': _L0_ffn_in['br']}

def reference(x, ctx_1024, L0_xattn_W_q, L0_xattn_b_q, L0_xattn_W_k, L0_xattn_b_k, L0_xattn_W_v, L0_xattn_b_v, L0_xattn_W_out, L0_xattn_b_out, L0_ffn_W1, L0_ffn_b1, L0_ffn_W2, L0_ffn_b2, L0_ffn_Wr, L0_ffn_br):
    import jax
    import jax.numpy as jnp

    def _L0_xattn_ref(x_q, x_kv, W_q, b_q, W_k, b_k, W_v, b_v, W_out, b_out):
        import jax, jax.numpy as jnp
        import numpy as np
        import math
        B, S, D, H = (4, 512, 256, 16)
        DH = D // H

        def _split_heads(x):
            b, s, _ = x.shape
            return x.reshape(b, s, H, DH).transpose(0, 2, 1, 3)
        q = x_q @ W_q.T + b_q
        k = x_kv @ W_k.T + b_k
        v = x_kv @ W_v.T + b_v
        qh, kh, vh = (_split_heads(q), _split_heads(k), _split_heads(v))
        scale = 1.0 / math.sqrt(DH)
        scores = jnp.einsum('bhqd,bhkd->bhqk', qh, kh) * scale
        attn = jax.nn.softmax(scores, axis=-1)
        ctx = jnp.einsum('bhqk,bhkd->bhqd', attn, vh)
        ctx = ctx.transpose(0, 2, 1, 3).reshape(x_q.shape[0], x_q.shape[1], D)
        return ctx @ W_out.T + b_out

    def _L0_ffn_ref(x, W1, b1, W2, b2, Wr, br):
        import jax, jax.numpy as jnp
        import numpy as np
        D = 256
        H = 512
        E = 8
        K = 2
        B, T = (4, 512)
        Bb, Tt, Dd = x.shape
        xf = x.reshape(-1, Dd)
        logits = xf @ Wr + br
        topk_val, topk_idx = jax.lax.top_k(logits, K)
        scores = jax.nn.softmax(topk_val, axis=-1)
        h = jnp.einsum('nd,edh->enh', xf, W1) + b1[:, None, :]
        a, g = jnp.split(h, 2, axis=-1)
        act = jax.nn.silu(a) * g
        out_e = jnp.einsum('enh,ehd->end', act, W2) + b2[:, None, :]
        out_ne = out_e.transpose(1, 0, 2)
        gathered = jnp.take_along_axis(out_ne, topk_idx[:, :, None], axis=1)
        out = jnp.sum(gathered * scores[:, :, None], axis=1)
        return out.reshape(Bb, Tt, Dd)
    x = x + _L0_xattn_ref(_layernorm(x, axis=-1), ctx_1024, L0_xattn_W_q, L0_xattn_b_q, L0_xattn_W_k, L0_xattn_b_k, L0_xattn_W_v, L0_xattn_b_v, L0_xattn_W_out, L0_xattn_b_out)
    x = x + _L0_ffn_ref(_layernorm(x, axis=-1), L0_ffn_W1, L0_ffn_b1, L0_ffn_W2, L0_ffn_b2, L0_ffn_Wr, L0_ffn_br)
    return x

_drawn_inputs = setup_inputs


def setup_inputs(seed=0):
    import zlib

    import numpy as np

    out = dict(_drawn_inputs(seed))
    spreads = {'L0_xattn_b_q': (0.0, 0.385),
     'L0_xattn_b_k': (0.0, 0.8),
     'L0_xattn_b_v': (0.0, 0.1),
     'L0_xattn_b_out': (0.0, 0.1),
     'L0_ffn_b1': (0.0, 0.8),
     'L0_ffn_b2': (0.0, 0.1),
     'L0_ffn_br': (0.0, 0.1)}
    factors = {'L0_ffn_W1': 3.476, 'L0_ffn_W2': 3.451}
    for name, (base, spread) in spreads.items():
        noise = np.random.default_rng([zlib.crc32(name.encode()), seed]).standard_normal(out[name].shape)
        drawn = base * np.exp(spread * noise) if base else spread * noise
        out[name] = jnp.asarray(drawn.astype(out[name].dtype))
    for name, factor in factors.items():
        out[name] = (out[name] * factor).astype(out[name].dtype)
    return out
```

```python
from contextlib import ExitStack

import concourse.bass as bass
from concourse import mybir

F32 = mybir.dt.float32
F32R = mybir.dt.float32r
BF16 = mybir.dt.bfloat16
I32 = mybir.dt.int32
U32 = mybir.dt.uint32
ALU = mybir.AluOpType
ACT = mybir.ActivationFunctionType
AX_X = mybir.AxisListType.X

P = 128
D = 256
KC = D // P
H = 16
DH = D // H
E = 8
TOPK = 2
F = 512
FC = F // P
EPS = 1e-5
SCALE = DH ** -0.5

GB = 4
LB = 8
HC = 4
NCH = H // HC
TERMS_Q = (0, 0, 1, 1, 0, 2)
TERMS_K = (0, 1, 0, 1, 2, 0)
SCG = 16 * GB * TOPK
NSTK = 2 * len(TERMS_Q)
KS = len(TERMS_Q) * DH
ROW = 272
TOK, GATE = D, D + 1

C_ID, C_TRI, C_ONE, C_I8, C_BASE, C_THR, C_BLK, C_T8, C_P, C_END = 0, 128, 256, 384, 392, 400, 464, 608, 672, 673


def sizes(NB):
    T = NB * P
    REG = T + P
    NBLK = (T * TOPK + E * (P - 1)) // P
    return T, REG, NBLK


def moe_layer(nc, x, ctx_in, wqT, wkT, wvT, woT, bq, bk, bv, bo, w1, b1, w2, b2, wr, br, cst, out):
    NB = x.shape[0]
    T, REG, NBLK = sizes(NB)
    NI = NB // LB
    assert NB % LB == 0 and NI >= 3

    xs = nc.dram_tensor("routed_rows", (E * REG + P, ROW), F32, kind="Internal").ap()

    outer = ExitStack()
    with outer:
        def sem(name):
            return outer.enter_context(nc.semaphore(name))

        bank = [outer.enter_context(nc.psum_tensor(f"bank{i}", [P, 512], F32)) for i in range(8)]
        consts = outer.enter_context(nc.sbuf_tensor("consts", [P, C_END], F32))
        cm = outer.enter_context(nc.sbuf_tensor("routed_before", [P, GB + 1, E], BF16))
        ones_bf = outer.enter_context(nc.sbuf_tensor("ones_bf", [P, P], BF16))
        s_const = sem("const_loaded")
        s_carry = sem("carry_added")
        ident = consts[:, C_ID:C_ID + P]

        attention(nc, sem, bank, consts, ident, ones_bf, cm, s_const, s_carry, NB, NI, REG, xs,
                  x, ctx_in, wqT, wkT, wvT, woT, bq, bk, bv, bo, wr, br, cst, out)
        if w1 is not None:
            experts(nc, sem, bank, consts, ident, ones_bf, cm, T, REG, NBLK, xs, w1, b1, w2, b2, out)


def attention(nc, sem, bank, consts, ident, ones_bf, cm, s_const, s_carry, NB, NI, REG, xs,
              x, ctx_in, wqT, wkT, wvT, woT, bq, bk, bv, bo, wr, br, cst, out):
    parts_dram = nc.dram_tensor("qk_parts_dram", (2, 3, KC, P, GB * P), BF16, kind="Internal").ap()

    def real(i, j):
        return not isinstance(i, int) or 0 <= LB * i + j < NB

    def count(i, j, per=1, done=None):
        return i * (LB * per) + (j * per + (per if done is None else done))

    def groups(i, j, per=1):
        return i * (LB // GB * per) + (j // GB + 1) * per

    def batch(i, j):
        return i * LB + j

    with ExitStack() as ctx:
        def sb(name, shape, dt):
            return ctx.enter_context(nc.sbuf_tensor(name, shape, dt))

        w_in = sb("w_in", [P, 4, KC, D], F32)
        w_hi = sb("w_hi", [P, 4, KC, D], F32R)
        w_lo = sb("w_lo", [P, 4, KC, D], F32R)
        bqk = sb("bqk", [P, 4], F32)
        bvb = sb("bv_rows", [P, D], F32)
        bob = sb("bo_rows", [P, D], F32)
        brb = sb("br_rows", [P, E], F32)
        wrs = sb("wr_sb", [P, KC, E], F32)
        tri_bf = sb("tri_bf", [P, P], BF16)
        id_bf = sb("id_bf", [P, P], BF16)
        mhalf = sb("minus_half", [P, 2], F32)

        x_in = sb("x_in", [P, GB, D], F32)
        c_in = sb("c_in", [P, GB, D], F32)
        xn = sb("xn", [P, GB, D], F32)
        st1 = sb("ln1_stats", [P, 2, 6], F32)
        mv1 = sb("ln1_mean_var", [P, 2, 2], F32)
        ve1 = sb("ln1_var_eps", [P, 2], F32)
        rs1 = sb("ln1_rstd", [P, 2], F32)
        t_hi = sb("t_hi", [P, 4, GB * P], F32R)
        t_lo = sb("t_lo", [P, 4, GB * P], F32R)
        parts = sb("qk_parts", [P, 4, 3, GB * P], BF16)
        rem = sb("qk_rem", [P, 2, GB * P], F32)
        qst = [sb(f"q_stack{i}", [P, H, GB * P], BF16) for i in range(2)]
        kst = [sb(f"k_stack{i}", [P, H, GB * P], BF16) for i in range(2)]
        va = sb("v_ones", [P, LB, H, 32], F32)
        mx = sb("row_max", [P, 2, H], F32)
        nm = sb("minus_max", [P, 2, H], BF16)
        nmT = sb("minus_max_T", [2 * H, 2, P], BF16)
        pT = sb("probs_T", [P, NCH, 512], F32)
        cu = sb("ctx_sums_T", [P, NCH, P], F32)
        rs = sb("recip_sum", [P, H], F32)
        cn = sb("ctx_norm", [P, D], F32)
        ch = sb("ctxT_hi", [P, KC, P], F32R)
        cl = sb("ctxT_lo", [P, KC, P], F32R)
        xres = sb("x_res", [P, 2, D], F32)
        xrb = sb("x_res_bo", [P, 2, D], F32)
        x2 = sb("x2", [P, 2, D], F32)
        st2 = sb("ln2_stats", [P, 6], F32)
        mv2 = sb("ln2_mean_var", [P, 2, 2], F32)
        ve2 = sb("ln2_var_eps", [P, 1], F32)
        rs2 = sb("ln2_rstd", [P, 2], F32)
        xr = sb("rows", [P, LB, ROW], F32)
        nT = sb("xn2_T", [P, KC, P], F32)
        lg = sb("logits", [P, LB, E], F32)
        mx8 = sb("top_vals", [P, GB, 8], F32)
        ix8 = sb("top_idx", [P, GB, 8], U32)
        ixf = sb("top_idx_f", [P, GB, TOPK], F32)
        oh = sb("onehot", [P, GB, TOPK, E], F32)
        mask = sb("mask", [P, GB, E], BF16)
        gd = sb("gate_diff", [P, GB], F32)
        ge = sb("gate_exp", [P, GB], F32)
        gden = sb("gate_den", [P, GB], F32)
        g12 = sb("gates", [P, GB, TOPK], F32)
        gg = sb("gates_oh", [P, GB, TOPK, E], F32)
        tpos = sb("rank_base", [P, GB, E], F32)
        dsel = sb("dest_sel", [P, GB, TOPK, E], F32)
        dstf = sb("dest_f", [P, GB, TOPK], F32)
        dsti = sb("dest_i", [P, 2, GB, TOPK], I32)
        tokf = sb("token_f", [P, LB], F32)

        s_w = sem("weights_loaded"); s_wh = sem("weights_hi"); s_wl = sem("weights_lo"); s_set = sem("setup_done")
        s_ldx = [sem(f"x_loaded{i}") for i in range(GB)]
        s_ldc = [sem(f"ctx_loaded{i}") for i in range(GB)]
        s_ldr = [sem(f"xres_loaded{i}") for i in range(2)]
        s_st1 = sem("ln1_stats_done"); s_mv1 = sem("ln1_mv_done"); s_ve1 = sem("ln1_ve_done")
        s_rs1 = sem("ln1_rstd_done"); s_xn = sem("ln1_done")
        s_xT = sem("xT_done"); s_xh = sem("xT_hi_done"); s_xl = sem("xT_lo_done")
        s_qk = sem("qk_proj_done"); s_p0 = sem("part0_done"); s_r = sem("rem_done"); s_p1 = sem("part1_done")
        s_p2 = sem("part2_done"); s_stk = sem("stacks_loaded"); s_prt = [sem(f"{w}_parts_stored") for w in "qk"]
        s_vm = sem("v_proj_done"); s_v = sem("v_done")
        s_s = sem("scores_done"); s_mx = sem("max_done"); s_nmh = sem("max_hi_done"); s_nm = sem("minus_max_done")
        s_mt = sem("max_T_done"); s_mT = sem("max_T_copied"); s_mrow = [sem(f"max_rows_loaded{i}") for i in range(2)]
        s_st = sem("scoresT_done"); s_exp = sem("exp_done"); s_pv = sem("pv_done"); s_cu = sem("ctx_copied")
        s_t1 = sem("ctx_tok_done"); s_rs = sem("recip_done"); s_cn = sem("ctx_norm_done")
        s_t2 = sem("ctx_T_done"); s_ch = sem("ctx_hi_done"); s_cl = sem("ctx_lo_done"); s_out = sem("out_proj_done")
        s_xb = sem("xres_bo_done"); s_x2 = sem("x2_done"); s_x2d = [sem(f"x2_stored{i}") for i in range(2)]
        s_st2 = sem("ln2_stats_done"); s_mv2 = sem("ln2_mv_done"); s_ve2 = sem("ln2_ve_done")
        s_rs2 = sem("ln2_rstd_done"); s_n2 = sem("ln2_done")
        s_t3 = sem("xn2_T_done"); s_nT = sem("xn2_T_copied"); s_lg = sem("logits_done"); s_lgt = sem("logits_copied")
        s_top = sem("top_vals_done"); s_ix = sem("top_idx_done"); s_ixf = sem("top_idx_f_done"); s_oh = sem("onehot_done")
        s_mask = sem("mask_done"); s_gd = sem("gate_diff_done"); s_ge = sem("gate_exp_done")
        s_gden = sem("gate_den_done"); s_g1 = sem("gate1_done"); s_g2 = sem("gate2_done"); s_gg = sem("gates_oh_done")
        s_rk = sem("rank_done"); s_tp = sem("rank_read"); s_dsel = sem("dest_sel_done"); s_dstf = sem("dest_f_done")
        s_route = sem("routing_done"); s_zero = sem("v_zeroed"); s_sc = sem("rows_scattered"); s_free = sem("row_buffers_free")
        s_took = {"dve": sem("dve_waits_taken"), "pool": sem("pool_waits_taken")}

        block = ctx.enter_context(nc.Block())

        def take(eng, name):
            eng.sem_inc(s_took[name], 1)

        def run(eng, slot, before):
            before()
            for j in range(LB):
                slot(0, j)
            with eng.Fori(1, NI - 1) as i:
                for j in range(LB):
                    slot(i, j)
            for j in range(LB):
                slot(NI - 1, j)
            for j in range(GB + 1):
                slot(NI, j)

        @block.sync
        def _(sp):
            def load_in(i, j):
                q = j % GB
                if real(i, j - GB):
                    sp.wait_ge(s_xn, groups(i, j - GB, 2) - (1 if q < 2 else 0))
                sp.dma_start(x_in[:, q, :], x[batch(i, j)]).then_inc(s_ldx[q], 16)
                if real(i, j - GB):
                    sp.wait_ge(s_xT, count(i, j - GB))
                sp.dma_start(c_in[:, q, :], ctx_in[batch(i, j)]).then_inc(s_ldc[q], 16)

            def load_stacks(i, j):
                par = (j // GB) % 2
                if real(i, j - 2 * GB):
                    sp.wait_ge(s_st, count(i, j - 2 * GB + GB - 1, NCH))
                for w in range(2):
                    for c in range(KC):
                        o = 2 * w + c
                        sp.wait_ge(s_p0, groups(i, j, 4) - 3 + o)
                        sp.dma_start(parts_dram[w, 0, c], parts[:, o, 0, :]).then_inc(s_prt[w], 16)
                        sp.wait_ge(s_p2, groups(i, j, 4) - 3 + o)
                        sp.dma_start(parts_dram[w, 1:3, c].rearrange("t p n -> p t n"), parts[:, o, 1:3, :]).then_inc(s_prt[w], 16)
                for w, (stack, terms) in enumerate(((qst, TERMS_Q), (kst, TERMS_K))):
                    sp.wait_ge(s_prt[w], groups(i, j, 16 * 2 * KC))
                    for s, part in enumerate(terms):
                        sp.dma_start(stack[par][DH * s:DH * (s + 1), :, :],
                                     parts_dram[w, part].rearrange("c (h d) n -> d (c h) n", d=DH)).then_inc(s_stk, 16)

            def before():
                sp.dma_start(consts[:], cst).then_inc(s_const, 16)
                for n, w in enumerate((wqT, wkT, wvT, woT)):
                    sp.dma_start(w_in[:, n], w.rearrange("(c p) n -> p c n", p=P)).then_inc(s_w, 16)
                sp.dma_start(wrs[:], wr.rearrange("(c p) e -> p c e", p=P)).then_inc(s_w, 16)
                for n, b in enumerate((bq, bq, bk, bk)):
                    c = n % 2
                    sp.dma_start(bqk[:, n:n + 1], b[c * P:(c + 1) * P].rearrange("(p o) -> p o", o=1)).then_inc(s_w, 16)
                for dst, b in ((bvb, bv), (bob, bo), (brb, br)):
                    sp.dma_start(dst[:], b.rearrange("(o n) -> o n", o=1).to_broadcast([P, b.shape[0]])).then_inc(s_w, 16)
                for q in range(GB):
                    load_in(0, q)
                load_stacks(0, 0)
                for q in range(GB):
                    load_in(0, GB + q)

            def slot(i, j):
                q = j % GB
                if real(i, j - 2):
                    jj = j - 2
                    if real(i, jj - 2):
                        sp.wait_ge(s_xb, count(i, jj - 2))
                    sp.dma_start(xres[:, jj % 2, :], x[batch(i, jj)]).then_inc(s_ldr[jj % 2], 16)
                if q in (2, 3):
                    for h in range(2):
                        later = (j // GB) * GB + 2 * GB + 2 * (q - 2) + h
                        if real(i, later):
                            load_in(i, later)
                if real(i, j - 3):
                    jj = j - 3
                    sp.wait_ge(s_x2, count(i, jj))
                    sp.dma_start(out[bass.ds(batch(i, jj) * P, P), :], x2[:, jj % 2, :]).then_inc(s_x2d[jj % 2], 16)
                if real(i, j):
                    par = (j // GB) % 2
                    sp.wait_ge(s_mT, count(i, j))
                    for part in range(2):
                        sp.dma_start(qst[par][KS + part:KS + part + 1, :, q * P:(q + 1) * P],
                                     nmT[H * part:H * (part + 1), j % 2, :]).then_inc(s_mrow[j % 2], 16)
                if q == 2 and real(i, j + GB):
                    load_stacks(i, (j // GB + 1) * GB)

            run(sp, slot, before)
            sp.wait_ge(s_x2d[0], 16 * (NB // 2))
            sp.wait_ge(s_x2d[1], 16 * (NB // 2))

        @block.tensor
        def _(pe):
            mm = nc.tensor.matmul

            def split3(dst, a_hi, a_lo, b_hi, b_lo):
                n = len(a_hi)
                for c in range(n):
                    mm(dst, a_hi[c], b_hi[c], start=(c == 0), stop=False)
                    mm(dst, a_hi[c], b_lo[c], start=False, stop=False)
                    last = mm(dst, a_lo[c], b_hi[c], start=False, stop=(c == n - 1))
                return last

            def to_T(i, j):
                q = j % GB
                if q % 2 == 0:
                    pe.wait_ge(s_xn, groups(i, j, 2) - (1 if q == 0 else 0))
                pe.wait_ge(s_ldc[q], groups(i, j, 16))
                if q == 0:
                    if real(i, j - 1):
                        pe.wait_ge(s_v, count(i, j - 1))
                else:
                    pe.wait_ge(s_xl, count(i, j - 1))
                for c in range(2 * KC):
                    src = (xn if c < KC else c_in)[:, q, (c % KC) * P:(c % KC + 1) * P]
                    last = nc.tensor.transpose(bank[5][:, c * P:(c + 1) * P], src, ident)
                last.then_inc(s_xT, 1)

            def qk_proj(i, j, pred_x2):
                pe.wait_ge(s_xl, count(i, j + GB - 1))
                for o in range(4):
                    w, c0, src = (0 if o < 2 else 1), (o % 2) * P, (0 if o < 2 else KC)
                    if o == 1 and pred_x2 is not None:
                        pe.wait_ge(s_x2, pred_x2)
                    if o >= 2:
                        pe.wait_ge(s_r, groups(i, j, 4) - 3 + o - 2)
                    split3(bank[5 if o % 2 == 0 else 7][:, :],
                           [w_hi[:, w, c, c0:c0 + P] for c in range(KC)], [w_lo[:, w, c, c0:c0 + P] for c in range(KC)],
                           [t_hi[:, src + c, :] for c in range(KC)], [t_lo[:, src + c, :] for c in range(KC)]
                           ).then_inc(s_qk, 1)

            def v_proj(i, j, pred_x2):
                for q in range(GB):
                    if q < 2:
                        pe.wait_ge(s_r, groups(i, j, 4) - 1 + q)
                        if q == 1 and pred_x2 is not None:
                            pe.wait_ge(s_x2, pred_x2)
                    else:
                        pe.wait_ge(s_v, count(i, j + q - 2))
                    sl = slice(q * P, (q + 1) * P)
                    split3(bank[5 if q % 2 == 0 else 7][:, 0:D],
                           [t_hi[:, KC + c, sl] for c in range(KC)], [t_lo[:, KC + c, sl] for c in range(KC)],
                           [w_hi[:, 2, c, :] for c in range(KC)], [w_lo[:, 2, c, :] for c in range(KC)]
                           ).then_inc(s_vm, 1)

            def scores(i, j, c):
                par, sl = (j // GB) % 2, slice((j % GB) * P, (j % GB + 1) * P)
                if c == 0 and j % GB == 0:
                    pe.wait_ge(s_stk, groups(i, j, 16 * NSTK))
                if c >= 2 or real(i, j - 1):
                    pe.wait_ge(s_mx, count(i, j, NCH, c - 1))
                for r in range(HC):
                    h = HC * c + r
                    last = mm(bank[c % 2][:, r * P:(r + 1) * P], qst[par][0:KS, h, sl], kst[par][0:KS, h, sl],
                              start=True, stop=True)
                last.then_inc(s_s, 1)

            def scores_T(i, j, c):
                par, sl = (j // GB) % 2, slice((j % GB) * P, (j % GB + 1) * P)
                if c == 0:
                    pe.wait_ge(s_mrow[j % 2], i * (LB // 2 * 32) + (j // 2 + 1) * 32)
                if c >= 2 or real(i, j - 1):
                    pe.wait_ge(s_exp, count(i, j, NCH, c - 1))
                for r in range(HC):
                    h = HC * c + r
                    last = mm(bank[2 + c % 2][:, r * P:(r + 1) * P], kst[par][0:KS + 2, h, sl],
                              qst[par][0:KS + 2, h, sl], start=True, stop=True)
                last.then_inc(s_st, 1)

            def pv(i, j, c):
                pe.wait_ge(s_exp, count(i, j, NCH, c + 1))
                if c == 0:
                    pe.wait_ge(s_v, count(i, j))
                    if real(i, j - 1):
                        pe.wait_ge(s_cu, count(i, j - 1))
                for r in range(HC):
                    last = mm(bank[4][32 * r:32 * r + 32, c * P:(c + 1) * P], va[:, j % LB, HC * c + r, :],
                              pT[:, c, r * P:(r + 1) * P], start=True, stop=True)
                last.then_inc(s_pv, 1)

            def bank6_free(i, j, readers):
                for s, lag in readers:
                    if real(i, j - lag):
                        pe.wait_ge(s, count(i, j - lag))
                        break

            def before():
                pe.wait_ge(s_const, 16)
                pe.wait_ge(s_wl, 1)
                pe.wait_ge(s_set, 1)
                for q in range(GB):
                    to_T(0, q)
                qk_proj(0, 0, None)
                v_proj(0, 0, None)
                pe.wait_ge(s_v, GB)

            def slot(i, j):
                q = j % GB
                if real(i, j - 2):
                    pe.wait_ge(s_cu, count(i, j - 2))
                    bank6_free(i, j, [(s_mT, 1), (s_lgt, 4)])
                    if q == 0 and real(i, j - 5):
                        pe.wait_ge(s_tp, groups(i, j - 5))
                    for c in range(NCH):
                        last = nc.tensor.transpose(bank[6][:, c * P:(c + 1) * P], cu[:, c, :], ident)
                    last.then_inc(s_t1, 1)
                for c in range(2):
                    if real(i, j):
                        scores(i, j, c)
                for c in range(2):
                    if real(i, j - 1):
                        scores_T(i, j - 1, c)
                if real(i, j - 3):
                    pe.wait_ge(s_n2, count(i, j - 3))
                    bank6_free(i, j, [(s_cn, 2), (s_mT, 1), (s_lgt, 4)])
                    for c in range(KC):
                        last = nc.tensor.transpose(bank[6][:, c * P:(c + 1) * P],
                                                   xr[:, (j - 3) % LB, c * P:(c + 1) * P], ident)
                    last.then_inc(s_t3, 1)
                if real(i, j - 1):
                    pv(i, j - 1, 0)
                if real(i, j - 2):
                    pe.wait_ge(s_cn, count(i, j - 2))
                    if real(i, j - 3):
                        pe.wait_ge(s_x2, count(i, j - 3))
                    if q == 3 and real(i, j + 1):
                        pe.wait_ge(s_r, groups(i, j + 1, 4))
                    if q == 0 and real(i, j):
                        pe.wait_ge(s_v, count(i, j + 3))
                    for c in range(KC):
                        last = nc.tensor.transpose(bank[7][:, c * P:(c + 1) * P], cn[:, c * P:(c + 1) * P], ident)
                    last.then_inc(s_t2, 1)
                if real(i, j):
                    scores(i, j, 2)
                if real(i, j - 1):
                    scores_T(i, j - 1, 2)
                    pv(i, j - 1, 1)
                if real(i, j - 3):
                    pe.wait_ge(s_nT, count(i, j - 3))
                    for c in range(KC):
                        last = mm(bank[6][:, 0:E], nT[:, c, :], wrs[:, c, :], start=(c == 0), stop=(c == KC - 1))
                    last.then_inc(s_lg, 1)
                if real(i, j):
                    scores(i, j, 3)
                if real(i, j - 1):
                    scores_T(i, j - 1, 3)
                    pv(i, j - 1, 2)
                if real(i, j - 2):
                    pe.wait_ge(s_cl, count(i, j - 2))
                    split3(bank[7][:, 0:D], [ch[:, c, :] for c in range(KC)], [cl[:, c, :] for c in range(KC)],
                           [w_hi[:, 3, c, :] for c in range(KC)], [w_lo[:, 3, c, :] for c in range(KC)]
                           ).then_inc(s_out, 1)
                if real(i, j):
                    pe.wait_ge(s_nm, count(i, j))
                    bank6_free(i, j, [(s_lgt, 3), (s_cn, 2), (s_mT, 1)])
                    nc.tensor.transpose(bank[6][0:2 * H, 0:P // 2].bitcast(BF16), nm[:].rearrange("p t h -> p (t h)"),
                                        id_bf[:]).then_inc(s_mt, 1)
                if real(i, j - 1):
                    pv(i, j - 1, 3)
                g1 = (j // GB + 1) * GB
                pred = count(i, j - 2) if real(i, j - 2) else None
                if real(i, j + GB):
                    if q < 2:
                        for h in range(2):
                            to_T(i, g1 + 2 * q + h)
                    elif q == 2:
                        qk_proj(i, g1, pred)
                    else:
                        v_proj(i, g1, pred)
                if q == 3 and real(i, j - 4):
                    pe.wait_ge(s_carry, groups(i, j - 4, GB + 1))
                    bank6_free(i, j, [(s_mT, 0), (s_lgt, 3), (s_lgt, 4)])
                    mm(bank[6][:, 0:GB * E], tri_bf[:], mask[:].rearrange("p b e -> p (b e)"), start=True, stop=False)
                    mm(bank[6][:, 0:GB * E], ones_bf[:], cm[:, 0:GB, :].rearrange("p b e -> p (b e)"),
                       start=False, stop=True).then_inc(s_rk, 1)

            run(pe, slot, before)

        @block.scalar
        def _(act):
            def xT_hi(i, j):
                q = j % GB
                act.wait_ge(s_xT, count(i, j))
                if q == 0 and real(i, j - 1):
                    act.wait_ge(s_vm, count(i, j - 1))
                nc.scalar.activation(t_hi[:, :, q * P:(q + 1) * P],
                                     bank[5][:, :].rearrange("p (c n) -> p c n", c=4), ACT.Copy).then_inc(s_xh, 1)

            def part0(i, j):
                if real(i, j - GB):
                    act.wait_ge(s_stk, groups(i, j - GB, 16 * NSTK))
                for o in range(4):
                    act.wait_ge(s_qk, groups(i, j, 4) - 3 + o)
                    nc.scalar.activation(parts[:, o, 0, :], bank[5 if o % 2 == 0 else 7][:, :], ACT.Identity,
                                         bias=bqk[:, o:o + 1]).then_inc(s_p0, 1)

            def exps(i, j, c):
                act.wait_ge(s_st, count(i, j, NCH, c + 1))
                if real(i, j - 1):
                    act.wait_ge(s_pv, count(i, j - 1, NCH, c + 1))
                nc.scalar.activation(pT[:, c, :], bank[2 + c % 2][:, :], ACT.Exp, scale=SCALE).then_inc(s_exp, 1)

            def before():
                act.wait_ge(s_w, 16 * 12)
                nc.scalar.activation(w_hi[:].rearrange("p a b c -> p (a b c)"), w_in[:].rearrange("p a b c -> p (a b c)"),
                                     ACT.Copy).then_inc(s_wh, 1)
                for q in range(GB):
                    xT_hi(0, q)
                part0(0, 0)

            def slot(i, j):
                q = j % GB
                for c in range(2):
                    if real(i, j - 1):
                        exps(i, j - 1, c)
                if real(i, j - 3):
                    act.wait_ge(s_t3, count(i, j - 3))
                    if real(i, j - 4):
                        act.wait_ge(s_lg, count(i, j - 4))
                    nc.scalar.activation(nT[:].rearrange("p c n -> p (c n)"), bank[6][:, 0:D], ACT.Copy).then_inc(s_nT, 1)
                if real(i, j - 2):
                    act.wait_ge(s_t2, count(i, j - 2))
                    if real(i, j - 3):
                        act.wait_ge(s_out, count(i, j - 3))
                    nc.scalar.activation(ch[:].rearrange("p c n -> p (c n)"), bank[7][:, 0:D], ACT.Copy).then_inc(s_ch, 1)
                for c in range(2, 4):
                    if real(i, j - 1):
                        exps(i, j - 1, c)
                if real(i, j):
                    act.wait_ge(s_mt, count(i, j))
                    if real(i, j - 2):
                        act.wait_ge(s_mrow[j % 2], i * (LB // 2 * 32) + (j // 2) * 32)
                    nc.scalar.activation(nmT[:, j % 2, :], bank[6][0:2 * H, 0:P // 2].bitcast(BF16),
                                         ACT.Copy).then_inc(s_mT, 1)
                if real(i, j - 1):
                    act.wait_ge(s_pv, count(i, j - 1, NCH))
                    if real(i, j - 2):
                        act.wait_ge(s_t1, count(i, j - 2))
                    nc.scalar.activation(cu[:].rearrange("p c n -> p (c n)"), bank[4][:, :], ACT.Copy).then_inc(s_cu, 1)
                g1 = (j // GB + 1) * GB
                if real(i, j + GB):
                    if q < 2:
                        for h in range(2):
                            xT_hi(i, g1 + 2 * q + h)
                    elif q == 2:
                        part0(i, g1)
                if q == 3 and real(i, j - 4):
                    act.wait_ge(s_gd, groups(i, j - 4))
                    nc.scalar.activation(ge[:], gd[:], ACT.Exp).then_inc(s_ge, 1)

            run(act, slot, before)

        @block.vector
        def _(dve):
            V = nc.vector

            def ln1_stats(i, j):
                n = groups(i, j, 2) - (1 if j % GB == 0 else 0)
                for h in range(2):
                    dve.wait_ge(s_ldx[j % GB + h], groups(i, j, 16))
                    V.bn_stats(st1[:, h, :], x_in[:, j % GB + h, :]).then_inc(s_st1, 1)
                dve.wait_ge(s_st1, 2 * n)
                take(dve, "dve")
                for h in range(2):
                    V.bn_aggr(mv1[:, h, :], st1[:, h, :]).then_inc(s_mv1, 1)
                dve.wait_ge(s_mv1, 2 * n)
                V.tensor_scalar(ve1[:], mv1[:, :, 1], EPS, None, ALU.add).then_inc(s_ve1, 1)

            def ln1_norm(i, j):
                n = groups(i, j, 2) - (1 if j % GB == 0 else 0)
                dve.wait_ge(s_rs1, n)
                for h in range(2):
                    if real(i, j + h - GB):
                        dve.wait_ge(s_xT, count(i, j + h - GB))
                    last = V.tensor_scalar(xn[:, j % GB + h, :], x_in[:, j % GB + h, :], mv1[:, h, 0:1], rs1[:, h:h + 1],
                                           ALU.subtract, ALU.mult)
                last.then_inc(s_xn, 1)

            def xT_lo(i, j):
                q = j % GB
                dve.wait_ge(s_xh, count(i, j))
                V.tensor_tensor(t_lo[:, :, q * P:(q + 1) * P], bank[5][:, :].rearrange("p (c n) -> p c n", c=4),
                                t_hi[:, :, q * P:(q + 1) * P].bitcast(F32), ALU.subtract).then_inc(s_xl, 1)

            def remainders(i, j):
                for o in range(4):
                    dve.wait_ge(s_p0, groups(i, j, 4) - 3 + o)
                    if o >= 2 or real(i, j - GB):
                        dve.wait_ge(s_p2, groups(i, j, 4) - 3 + o - 2)
                    V.scalar_tensor_tensor(rem[:, o % 2, :], bank[5 if o % 2 == 0 else 7][:, :], bqk[:, o:o + 1],
                                           parts[:, o, 0, :], ALU.add, ALU.subtract).then_inc(s_r, 1)

            def v_rows(i, j):
                for q in range(GB):
                    dve.wait_ge(s_vm, count(i, j + q))
                    if real(i, j + q - LB):
                        dve.wait_ge(s_pv, count(i, j + q - LB, NCH))
                    V.tensor_tensor(va[:, (j + q) % LB, :, 0:DH],
                                    bank[5 if q % 2 == 0 else 7][:, 0:D].rearrange("p (h d) -> p h d", h=H),
                                    bvb[:].rearrange("p (h d) -> p h d", h=H), ALU.add).then_inc(s_v, 1)

            def maxima(i, j, c):
                dve.wait_ge(s_s, count(i, j, NCH, c + 1))
                V.tensor_reduce(mx[:, j % 2, HC * c:HC * (c + 1)], bank[c % 2][:, :].rearrange("p (h k) -> p h k", h=HC),
                                AX_X, ALU.max).then_inc(s_mx, 1)

            def route1(i, j):
                n = groups(i, j)
                b0 = j % LB
                dve.wait_ge(s_lgt, count(i, j + GB - 1))
                take(dve, "dve")
                for q in range(GB):
                    V.max(mx8[:, q, :], lg[:, b0 + q, :]).then_inc(s_top, 1)
                dve.wait_ge(s_top, n * GB)
                take(dve, "dve")
                for q in range(GB):
                    V.max_index(ix8[:, q, :], mx8[:, q, :], lg[:, b0 + q, :]).then_inc(s_ix, 1)
                V.tensor_tensor(gd[:], mx8[:, :, 1], mx8[:, :, 0], ALU.subtract).then_inc(s_gd, 1)
                dve.wait_ge(s_ix, n * GB)
                V.tensor_copy(ixf[:], ix8[:, :, 0:TOPK]).then_inc(s_ixf, 1)
                dve.wait_ge(s_ixf, n)
                for k in range(TOPK):
                    last = V.tensor_tensor(oh[:, :, k, :], ixf[:, :, k:k + 1].to_broadcast([P, GB, E]),
                                           consts[:, C_I8:C_I8 + E].rearrange("p (o e) -> p o e", o=1).to_broadcast([P, GB, E]),
                                           ALU.is_equal)
                last.then_inc(s_oh, 1)
                dve.wait_ge(s_oh, n)
                V.tensor_tensor(mask[:], oh[:, :, 0, :], oh[:, :, 1, :], ALU.add).then_inc(s_mask, 1)
                dve.wait_ge(s_mask, n)
                V.tensor_copy(cm[:, 0, :], cm[:, GB, :]).then_inc(s_carry, 1)
                for q in range(GB):
                    dve.wait_ge(s_carry, groups(i, j, GB + 1) - (GB - q))
                    V.tensor_tensor(cm[:, q + 1, :], cm[:, q, :], mask[:, q, :], ALU.add).then_inc(s_carry, 1)
                dve.wait_ge(s_carry, groups(i, j, GB + 1))

            def route2(i, j):
                n = groups(i, j)
                b0, par = j % LB, (j // GB) % 2
                dve.wait_ge(s_rk, n)
                V.tensor_tensor(tpos[:], bank[6][:, 0:GB * E].rearrange("p (b e) -> p b e", b=GB),
                                consts[:, C_BASE:C_BASE + E].rearrange("p (o e) -> p o e", o=1).to_broadcast([P, GB, E]),
                                ALU.add).then_inc(s_tp, 1)
                dve.wait_ge(s_ge, n)
                V.tensor_scalar(gden[:], ge[:], 1.0, None, ALU.add).then_inc(s_gden, 1)
                dve.wait_ge(s_gden, n)
                V.reciprocal(g12[:, :, 0], gden[:]).then_inc(s_g1, 1)
                dve.wait_ge(s_g1, n)
                V.tensor_tensor(g12[:, :, 1], g12[:, :, 0], ge[:], ALU.mult).then_inc(s_g2, 1)
                dve.wait_ge(s_tp, n)
                for k in range(TOPK):
                    V.tensor_tensor(dsel[:, :, k, :], oh[:, :, k, :], tpos[:], ALU.mult).then_inc(s_dsel, 1)
                dve.wait_ge(s_dsel, TOPK * n)
                V.tensor_reduce(dstf[:], dsel[:], AX_X, ALU.add).then_inc(s_dstf, 1)
                dve.wait_ge(s_g2, n)
                for k in range(TOPK):
                    V.tensor_tensor(gg[:, :, k, :], oh[:, :, k, :], g12[:, :, k:k + 1].to_broadcast([P, GB, E]),
                                    ALU.mult).then_inc(s_gg, 1)
                dve.wait_ge(s_dstf, n)
                if real(i, j - 2 * GB):
                    dve.wait_ge(s_free, groups(i, j - 2 * GB) + 2)
                V.tensor_copy(dsti[:, par], dstf[:])
                dve.wait_ge(s_gg, TOPK * n)
                V.tensor_tensor(xr[:, b0:b0 + GB, GATE:GATE + E], gg[:, :, 0, :], gg[:, :, 1, :], ALU.add)
                V.tensor_copy(xr[:, b0:b0 + GB, TOK].bitcast(I32), tokf[:, b0:b0 + GB]).then_inc(s_route, 1)
                V.tensor_scalar(tokf[:, b0:b0 + GB], tokf[:, b0:b0 + GB], float(LB * P), None, ALU.add)

            def before():
                dve.sem_inc(s_free, 2)
                V.memset(va[:].rearrange("p b h d -> p (b h d)"), 0.0).then_inc(s_zero, 1)
                dve.wait_ge(s_zero, 1)
                V.memset(va[:, :, :, DH:DH + 1], 1.0)
                V.memset(mhalf[:], -0.5)
                V.memset(cm[:, GB, :], 0.0)
                V.memset(ones_bf[:], 1.0)
                for k in range(2):
                    V.memset(kst[k][KS:KS + 2, :, :].rearrange("p h n -> p (h n)"), 1.0)
                V.memset(xr[:, :, GATE + E:ROW], 0.0)
                dve.wait_ge(s_const, 16)
                V.tensor_copy(tri_bf[:], consts[:, C_TRI:C_TRI + P])
                V.tensor_copy(id_bf[:], ident)
                for b in range(LB):
                    last = V.tensor_scalar(tokf[:, b:b + 1], consts[:, C_P:C_P + 1], float(P * b), None, ALU.add)
                last.then_inc(s_set, 1)
                dve.wait_ge(s_wh, 1)
                V.tensor_tensor(w_lo[:].rearrange("p a b c -> p (a b c)"), w_in[:].rearrange("p a b c -> p (a b c)"),
                                w_hi[:].rearrange("p a b c -> p (a b c)").bitcast(F32), ALU.subtract).then_inc(s_wl, 1)
                for h in range(2):
                    ln1_stats(0, 2 * h)
                    ln1_norm(0, 2 * h)
                for q in range(GB):
                    xT_lo(0, q)
                remainders(0, 0)
                v_rows(0, 0)

            def slot(i, j):
                q = j % GB
                g1 = (j // GB + 1) * GB
                if q == 0 and real(i, j - 5):
                    route2(i, j - 2 * GB)
                if real(i, j - 3):
                    jj = j - 3
                    dve.wait_ge(s_rs2, count(i, jj))
                    if real(i, jj - LB):
                        dve.wait_ge(s_free, groups(i, jj - LB) + 2)
                    V.tensor_scalar(xr[:, jj % LB, 0:D], x2[:, jj % 2, :], mv2[:, jj % 2, 0:1], rs2[:, jj % 2:jj % 2 + 1],
                                    ALU.subtract, ALU.mult).then_inc(s_n2, 1)
                if real(i, j - 2):
                    psv = bank[6][:, :].rearrange("p (h d) -> p h d", h=H)
                    dve.wait_ge(s_t1, count(i, j - 2))
                    V.reciprocal(rs[:], psv[:, :, DH]).then_inc(s_rs, 1)
                    dve.wait_ge(s_rs, count(i, j - 2))
                    if real(i, j - 3):
                        dve.wait_ge(s_t2, count(i, j - 3))
                    V.tensor_tensor(cn[:].rearrange("p (h d) -> p h d", h=H), psv[:, :, 0:DH],
                                    rs[:].rearrange("p (h o) -> p h o", o=1).to_broadcast([P, H, DH]), ALU.mult).then_inc(s_cn, 1)
                if real(i, j):
                    maxima(i, j, 0)
                    maxima(i, j, 1)
                if q < 2 and real(i, j + GB):
                    ln1_stats(i, g1 + 2 * q)
                if real(i, j - 2):
                    dve.wait_ge(s_ch, count(i, j - 2))
                    V.tensor_tensor(cl[:].rearrange("p c n -> p (c n)"), bank[7][:, 0:D],
                                    ch[:].rearrange("p c n -> p (c n)").bitcast(F32), ALU.subtract).then_inc(s_cl, 1)
                if real(i, j):
                    maxima(i, j, 2)
                if real(i, j - 3):
                    dve.wait_ge(s_lg, count(i, j - 3))
                    V.tensor_tensor(lg[:, (j - 3) % LB, :], bank[6][:, 0:E], brb[:], ALU.add).then_inc(s_lgt, 1)
                if q < 2 and real(i, j + GB):
                    ln1_norm(i, g1 + 2 * q)
                if real(i, j):
                    maxima(i, j, 3)
                    dve.wait_ge(s_mx, count(i, j, NCH))
                    if real(i, j - 1):
                        dve.wait_ge(s_mt, count(i, j - 1))
                    V.tensor_scalar(nm[:, 0, :], mx[:, j % 2, :], -1.0, None, ALU.mult).then_inc(s_nmh, 1)
                    dve.wait_ge(s_nmh, count(i, j))
                    V.scalar_tensor_tensor(nm[:, 1, :], mx[:, j % 2, :], -1.0, nm[:, 0, :], ALU.mult,
                                           ALU.subtract).then_inc(s_nm, 1)
                if real(i, j - 2):
                    jj = j - 2
                    dve.wait_ge(s_out, count(i, jj))
                    dve.wait_ge(s_xb, count(i, jj))
                    if real(i, jj - 2):
                        dve.wait_ge(s_x2d[jj % 2], i * (LB // 2 * 16) + (jj // 2) * 16)
                    V.tensor_tensor(x2[:, jj % 2, :], bank[7][:, 0:D], xrb[:, jj % 2, :], ALU.add).then_inc(s_x2, 1)
                    dve.wait_ge(s_x2, count(i, jj))
                    V.bn_stats(st2[:], x2[:, jj % 2, :]).then_inc(s_st2, 1)
                    dve.wait_ge(s_st2, count(i, jj))
                    take(dve, "dve")
                    V.bn_aggr(mv2[:, jj % 2, :], st2[:]).then_inc(s_mv2, 1)
                    dve.wait_ge(s_mv2, count(i, jj))
                    if real(i, jj - 1):
                        dve.wait_ge(s_rs2, count(i, jj - 1))
                    V.tensor_scalar(ve2[:], mv2[:, jj % 2, 1:2], EPS, None, ALU.add).then_inc(s_ve2, 1)
                if real(i, j + GB):
                    if q < 2:
                        for h in range(2):
                            xT_lo(i, g1 + 2 * q + h)
                    elif q == 2:
                        remainders(i, g1)
                    else:
                        v_rows(i, g1)
                if q == 3 and real(i, j - 4):
                    route1(i, j - 3 - GB)

            run(dve, slot, before)

        @block.gpsimd
        def _(pool):
            G = nc.gpsimd

            def parts12(i, j):
                for o in range(4):
                    n = groups(i, j, 4) - 3 + o
                    pool.wait_ge(s_r, n)
                    if o == 0 and real(i, j - GB):
                        pool.wait_ge(s_stk, groups(i, j - GB, 16 * NSTK))
                    take(pool, "pool")
                    G.tensor_copy(parts[:, o, 1, :], rem[:, o % 2, :]).then_inc(s_p1, 1)
                    pool.wait_ge(s_p1, n)
                    G.tensor_tensor(parts[:, o, 2, :], rem[:, o % 2, :], parts[:, o, 1, :], ALU.subtract).then_inc(s_p2, 1)

            def rstd1(i, j):
                n = groups(i, j, 2) - (1 if j % GB == 0 else 0)
                pool.wait_ge(s_ve1, n)
                if n is not None and (not isinstance(n, int) or n > 1):
                    pool.wait_ge(s_xn, n - 1)
                G.tensor_tensor(rs1[:], ve1[:], mhalf[:], ALU.pow).then_inc(s_rs1, 1)

            def before():
                pool.wait_ge(s_set, 1)
                pool.wait_ge(s_w, 16 * 12)
                rstd1(0, 0)
                rstd1(0, 2)
                parts12(0, 0)

            def slot(i, j):
                q = j % GB
                g1 = (j // GB + 1) * GB
                if q == 0 and real(i, j - 5):
                    jj = j - 2 * GB
                    par, b0 = (jj // GB) % 2, jj % LB
                    pool.wait_ge(s_route, groups(i, jj))
                    take(pool, "pool")
                    for b in range(GB):
                        for k in range(TOPK):
                            G.indirect_dma_start(out=xs[:, :],
                                                 out_offset=bass.IndirectOffsetOnAxis(ap=dsti[:, par, b, k:k + 1], axis=0),
                                                 in_=xr[:, b0 + b, :], in_offset=None).then_inc(s_sc, 16)
                if real(i, j - 2):
                    jj = j - 2
                    pool.wait_ge(s_ldr[jj % 2], i * (LB // 2 * 16) + (jj // 2 + 1) * 16)
                    if real(i, jj - 2):
                        pool.wait_ge(s_x2, count(i, jj - 2))
                    G.tensor_tensor(xrb[:, jj % 2, :], xres[:, jj % 2, :], bob[:], ALU.add).then_inc(s_xb, 1)
                if q < 2 and real(i, j + GB):
                    rstd1(i, g1 + 2 * q)
                if real(i, j - 2):
                    jj = j - 2
                    pool.wait_ge(s_ve2, count(i, jj))
                    if real(i, jj - 2):
                        pool.wait_ge(s_n2, count(i, jj - 2))
                    G.tensor_tensor(rs2[:, jj % 2:jj % 2 + 1], ve2[:], mhalf[:, 0:1], ALU.pow).then_inc(s_rs2, 1)
                if q == 2 and real(i, j - 7):
                    pool.wait_ge(s_sc, groups(i, j - 2 * GB, SCG))
                    pool.sem_inc(s_free, 1)
                if q == 2 and real(i, j + GB):
                    parts12(i, g1)

            run(pool, slot, before)
            pool.wait_ge(s_sc, 16 * TOPK * NB)


def experts(nc, sem, bank, consts, ident, ones_bf, cm, T, REG, NBLK, xs, w1, b1, w2, b2, out):
    U = 4
    NT = (NBLK + U - 1) // U * U
    NTH = T // P
    NB1 = E * 2 * F
    with ExitStack() as ctx:
        def sb(name, shape, dt):
            return ctx.enter_context(nc.sbuf_tensor(name, shape, dt))

        w1h = sb("w1_hi", [P, E * KC * 2 * F], F32R)
        w1l = sb("w1_lo", [P, E * KC * 2 * F], F32R)
        w2s = sb("w2_sb", [P, E * FC * D], F32)
        bp = sb("bias_parts", [P, NB1 + E * D], BF16)
        stage = sb("stage", [P, 2, 2 * F], F32)
        bsp = sb("bias_split", [P, NB1 // P + E * D // P], F32)
        bpt = sb("bias_part_tiles", [P, 3, NB1 // P + E * D // P], BF16)
        sel3 = sb("three_ones", [P, P], BF16)
        cnt = sb("counts", [P, E], F32)
        nbk = sb("blocks_of", [P, E], F32)
        incl = sb("blocks_upto", [P, E], F32)
        flat = stage[0:1, :, :].rearrange("p a n -> p (a n)")
        ej, st = (flat[:, (E + k) * NT:(E + k + 1) * NT] for k in range(2))
        tab = sb("tables", [1, 2, NT], I32)
        prow = sb("idle_at", [1, E], I32)
        prf = sb("idle_at_f", [1, E], F32)
        xb = sb("block_rows", [P, 2, ROW], F32)
        tk = sb("block_tokens", [P, U], I32)
        gt = sb("block_gates", [P, U], F32)
        pad = xb[:, 1, :]
        xh = sb("block_T_hi", [P, 2, KC * P], F32R)
        xl = sb("block_T_lo", [P, 2, KC * P], F32R)
        sa = sb("silu_a", [P, F], F32)
        ac = sb("act", [P, F], F32)
        aT = sb("act_T", [P, FC, P], F32)
        yg = sb("y_gated", [P, 2, D], F32)

        s_cnt = sem("counts_summed"); s_t = sem("table_step"); s_tab = sem("tables_done")
        s_bl = sem("biases_loaded"); s_bs = sem("bias_step"); s_bd = sem("bias_parts_placed"); s_zb = sem("bias_zeroed")
        s_w2 = sem("w2_loaded"); s_wst = [sem(f"w1_staged{k}") for k in range(2)]
        s_w1h = sem("w1_hi_done"); s_w1l = sem("w1_lo_done")
        s_pad = sem("idle_rows_ready"); s_pd = sem("idle_rows_stored")
        s_ld = [sem(f"block_loaded{k}") for k in range(2)]
        s_meta = sem("block_meta_read"); s_xT = sem("block_T_done"); s_xh = sem("block_hi_done"); s_xl = sem("block_lo_done")
        s_a = sem("w1a_done"); s_g = sem("w1g_done"); s_sa = sem("silu_done"); s_ac = sem("act_done")
        s_at = sem("act_T_done"); s_aT = sem("act_T_copied"); s_y = sem("w2_done"); s_yg = sem("y_gated_done")
        s_add = sem("rows_added"); s_turn = sem("add_turns")

        block = ctx.enter_context(nc.Block())

        def turns(eng, first, slot, last):
            first()
            for u in range(U):
                slot(0, u)
            with eng.Fori(1, NT // U - 1) as i:
                for u in range(U):
                    slot(i, u)
            for u in range(U):
                slot(NT // U - 1, u)
            last(NT // U)

        def blk(i, u):
            return i * U + u

        def real(i, u):
            return not isinstance(i, int) or 0 <= i * U + u < NT

        def n(i, u):
            return i * U + (u + 1)

        def n2(i, u):
            return i * (U // 2 * 16) + (u // 2 + 1) * 16

        @block.sync
        def _(sp):
            sp.dma_start(bsp[:, 0:NB1 // P], b1.rearrange("e n -> (e n)").rearrange("(p n) -> p n", p=P)).then_inc(s_bl, 16)
            sp.dma_start(bsp[:, NB1 // P:], b2.rearrange("e n -> (e n)").rearrange("(p n) -> p n", p=P)).then_inc(s_bl, 16)
            for k in range(E * KC):
                e, c = k // KC, k % KC
                if k == 0:
                    sp.wait_ge(s_tab, 1)
                if k >= 2:
                    sp.wait_ge(s_w1l, k - 1)
                sp.dma_start(stage[:, k % 2, :], w1[e, c * P:(c + 1) * P, :]).then_inc(s_wst[k % 2], 16)
                if k == 0:
                    sp.wait_ge(s_pad, 1)
                    for ee in range(E):
                        r = sp.value_load(prow[0:1, ee:ee + 1], min_val=0, max_val=E * REG - P)
                        sp.dma_start(xs[bass.ds(r, P), :], pad).then_inc(s_pd, 16)
                    sp.dma_start(xs[E * REG:E * REG + P, :], pad).then_inc(s_pd, 16)
                    sp.dma_start(out[T:T + P, :], pad[:, 0:D]).then_inc(s_pd, 16)
                if c == KC - 1:
                    sp.dma_start(w2s[:, e * FC * D:(e + 1) * FC * D].rearrange("p (c n) -> p c n", c=FC),
                                 w2[e].rearrange("(c p) n -> p c n", p=P)).then_inc(s_w2, 16)
            sp.wait_ge(s_bs, 5)
            sp.wait_ge(s_zb, 1)
            for k in range(3):
                sp.dma_start(bp[k:k + 1, 0:NB1].rearrange("o (p n) -> o p n", p=P),
                             bpt[:, k, 0:NB1 // P]).then_inc(s_bd, 16)
                sp.dma_start(bp[k:k + 1, NB1:].rearrange("o (p n) -> o p n", p=P),
                             bpt[:, k, NB1 // P:]).then_inc(s_bd, 16)
            sp.wait_ge(s_pd, 16 * (E + 2))

            def slot(i, u):
                if real(i, u - 2):
                    sp.wait_ge(s_xT, n(i, u - 2))
                    sp.wait_ge(s_meta, n(i, u - 2))
                r = sp.value_load(tab[0:1, 1, bass.ds(blk(i, u), 1)], min_val=0, max_val=E * REG)
                sp.dma_start(xb[:, u % 2, :], xs[bass.ds(r, P), :]).then_inc(s_ld[u % 2], 16)

            turns(sp, lambda: None, slot, lambda i: None)

        @block.tensor
        def _(pe):
            mm = nc.tensor.matmul
            pe.wait_ge(s_zb, 2)
            mm(bank[0][:, 0:E], ones_bf[:], cm[:, GB, :], start=True, stop=True).then_inc(s_cnt, 1)
            pe.wait_ge(s_w1l, E * KC)
            pe.wait_ge(s_w2, 16 * E)
            pe.wait_ge(s_bd, 16 * 6)

            def to_T(i, u):
                pe.wait_ge(s_ld[u % 2], n2(i, u))
                if real(i, u - 1):
                    pe.wait_ge(s_xl, n(i, u - 1))
                for c in range(KC):
                    last = nc.tensor.transpose(bank[4][:, c * P:(c + 1) * P], xb[:, u % 2, c * P:(c + 1) * P], ident)
                last.then_inc(s_xT, 1)

            def up(i, u, e, half):
                bk = bank[2 * (u % 2) + half]
                for c in range(KC):
                    h, l = (t[:, u % 2, c * P:(c + 1) * P] for t in (xh, xl))
                    at = e * (KC * 2 * F) + (c * 2 * F + half * F)
                    mm(bk[:, :], h, w1h[:, bass.ds(at, F)], start=(c == 0), stop=False)
                    mm(bk[:, :], h, w1l[:, bass.ds(at, F)], start=False, stop=False)
                    mm(bk[:, :], l, w1h[:, bass.ds(at, F)], start=False, stop=False)
                return mm(bk[:, :], sel3[:], bp[:, bass.ds(e * (2 * F) + half * F, F)], start=False, stop=True)

            def act_T(i, u):
                pe.wait_ge(s_ac, n(i, u))
                if real(i, u - 1):
                    pe.wait_ge(s_aT, n(i, u - 1))
                for c in range(FC):
                    last = nc.tensor.transpose(bank[5][:, c * P:(c + 1) * P], ac[:, c * P:(c + 1) * P], ident)
                last.then_inc(s_at, 1)

            def down(i, u, e):
                pe.wait_ge(s_aT, n(i, u))
                if real(i, u - 2):
                    pe.wait_ge(s_yg, n(i, u - 2))
                bk = bank[6 + u % 2]
                for c in range(FC):
                    mm(bk[:, 0:D], aT[:, c, :], w2s[:, bass.ds(e * (FC * D) + c * D, D)], start=(c == 0), stop=False)
                mm(bk[:, 0:D], sel3[:], bp[:, bass.ds(e * D + NB1, D)], start=False, stop=True).then_inc(s_y, 1)

            def expert(i, u):
                return pe.value_load(tab[0:1, 0, bass.ds(blk(i, u), 1)], min_val=0, max_val=E - 1)

            def slot(i, u):
                if real(i, u - 1):
                    act_T(i, u - 1)
                if real(i, u + 1):
                    to_T(i, u + 1)
                pe.wait_ge(s_xl, n(i, u))
                e = expert(i, u)
                if real(i, u - 2):
                    pe.wait_ge(s_sa, n(i, u - 2))
                up(i, u, e, 0).then_inc(s_a, 1)
                if real(i, u - 2):
                    pe.wait_ge(s_ac, n(i, u - 2))
                up(i, u, e, 1).then_inc(s_g, 1)
                if real(i, u - 1):
                    down(i, u - 1, expert(i, u - 1))

            def last(i):
                act_T(i, -1)
                down(i, -1, expert(i, -1))

            turns(pe, lambda: to_T(0, 0), slot, last)

        @block.scalar
        def _(act):
            for k in range(E * KC):
                act.wait_ge(s_wst[k % 2], 16 * (k // 2 + 1))
                nc.scalar.activation(w1h[:, k * 2 * F:(k + 1) * 2 * F], stage[:, k % 2, :], ACT.Copy).then_inc(s_w1h, 1)

            def x_hi(i, u):
                act.wait_ge(s_xT, n(i, u))
                if real(i, u - 2):
                    act.wait_ge(s_g, n(i, u - 2))
                nc.scalar.activation(xh[:, u % 2, :], bank[4][:, 0:D], ACT.Copy).then_inc(s_xh, 1)

            def slot(i, u):
                if real(i, u - 1):
                    act.wait_ge(s_at, n(i, u - 1))
                    if real(i, u - 2):
                        act.wait_ge(s_y, n(i, u - 2))
                    nc.scalar.activation(aT[:].rearrange("p c n -> p (c n)"), bank[5][:, :], ACT.Copy).then_inc(s_aT, 1)
                if real(i, u + 1):
                    x_hi(i, u + 1)
                act.wait_ge(s_a, n(i, u))
                if real(i, u - 1):
                    act.wait_ge(s_ac, n(i, u - 1))
                nc.scalar.activation(sa[:], bank[2 * (u % 2)][:, :], ACT.Silu).then_inc(s_sa, 1)

            def last(i):
                act.wait_ge(s_at, n(i, -1))
                act.wait_ge(s_y, n(i, -2))
                nc.scalar.activation(aT[:].rearrange("p c n -> p (c n)"), bank[5][:, :], ACT.Copy).then_inc(s_aT, 1)

            turns(act, lambda: x_hi(0, 0), slot, last)

        @block.vector
        def _(dve):
            V = nc.vector
            V.memset(bp[:].bitcast(U32), 0).then_inc(s_zb, 1)
            V.memset(sel3[:], 0.0).then_inc(s_t, 1)
            V.memset(pad, 0.0).then_inc(s_t, 1)
            dve.wait_ge(s_t, 2)
            V.memset(sel3[0:3, :], 1.0).then_inc(s_zb, 1)
            steps = [2]

            def step(ins):
                steps[0] += 1
                ins.then_inc(s_t, 1)
                dve.wait_ge(s_t, steps[0])

            V.tensor_scalar(pad[:, TOK:TOK + 1].bitcast(I32), consts[:, C_P:C_P + 1], float(T), None, ALU.add)
            dve.wait_ge(s_cnt, 1)
            step(V.tensor_copy(cnt[:], bank[0][:, 0:E]))
            scr = stage[:, 0, 0:E * NTH].rearrange("p (e k) -> p e k", e=E)
            step(V.tensor_tensor(scr, cnt[:].rearrange("p (e o) -> p e o", o=1).to_broadcast([P, E, NTH]),
                                 consts[:, C_THR:C_THR + NTH].rearrange("p (o k) -> p o k", o=1).to_broadcast([P, E, NTH]),
                                 ALU.is_gt))
            step(V.tensor_reduce(nbk[:], scr, AX_X, ALU.add))
            scr = stage[:, 0, 0:E * E].rearrange("p (e k) -> p e k", e=E)
            step(V.tensor_tensor(scr, consts[:, C_T8:C_T8 + E * E].rearrange("p (e k) -> p e k", e=E),
                                 nbk[:].rearrange("p (o k) -> p o k", o=1).to_broadcast([P, E, E]), ALU.mult))
            step(V.tensor_reduce(incl[:], scr, AX_X, ALU.add))
            scr = flat[:, 0:NT * E].rearrange("p (b e) -> p b e", e=E)
            step(V.tensor_tensor(scr, consts[0:1, C_BLK:C_BLK + NT].rearrange("p (b o) -> p b o", o=1).to_broadcast([1, NT, E]),
                                 incl[0:1, :].rearrange("p (o e) -> p o e", o=1).to_broadcast([1, NT, E]), ALU.is_ge))
            step(V.tensor_reduce(ej, scr, AX_X, ALU.add))
            step(V.tensor_tensor(scr, scr, nbk[0:1, :].rearrange("p (o e) -> p o e", o=1).to_broadcast([1, NT, E]), ALU.mult))
            step(V.tensor_reduce(st, scr, AX_X, ALU.add))
            step(V.tensor_tensor(st, consts[0:1, C_BLK:C_BLK + NT], st, ALU.subtract))
            step(V.tensor_scalar(st, st, float(P), None, ALU.mult))
            step(V.scalar_tensor_tensor(st, ej, float(REG), st, ALU.mult, ALU.add))
            step(V.tensor_scalar(tab[:, 1, :], st, float(E * REG), None, ALU.min))
            step(V.tensor_scalar(tab[:, 0, :], ej, float(E - 1), None, ALU.min))
            step(V.tensor_tensor(prf[:], cnt[0:1, :], consts[0:1, C_BASE:C_BASE + E], ALU.add))
            V.tensor_copy(prow[:], prf[:]).then_inc(s_tab, 1)
            dve.wait_ge(s_tab, 1)
            dve.sem_inc(s_pad, 1)
            for k in range(E * KC):
                dve.wait_ge(s_w1h, k + 1)
                V.tensor_tensor(w1l[:, k * 2 * F:(k + 1) * 2 * F], stage[:, k % 2, :],
                                w1h[:, k * 2 * F:(k + 1) * 2 * F].bitcast(F32), ALU.subtract).then_inc(s_w1l, 1)
            dve.wait_ge(s_bl, 32)
            bsteps = [0]

            def bstep(ins):
                bsteps[0] += 1
                ins.then_inc(s_bs, 1)
                dve.wait_ge(s_bs, bsteps[0])

            bstep(V.tensor_copy(bpt[:, 0, :], bsp[:]))
            bstep(V.tensor_tensor(bsp[:], bsp[:], bpt[:, 0, :], ALU.subtract))
            bstep(V.tensor_copy(bpt[:, 1, :], bsp[:]))
            bstep(V.tensor_tensor(bsp[:], bsp[:], bpt[:, 1, :], ALU.subtract))
            bstep(V.tensor_copy(bpt[:, 2, :], bsp[:]))

            def x_lo(i, u):
                dve.wait_ge(s_xh, n(i, u))
                V.tensor_tensor(xl[:, u % 2, :], bank[4][:, 0:D], xh[:, u % 2, :].bitcast(F32), ALU.subtract).then_inc(s_xl, 1)
                if real(i, u - U):
                    dve.wait_ge(s_add, i * (U * 16) + (u - U + 1) * 16)
                V.tensor_copy(tk[:, u % U:u % U + 1], xb[:, u % 2, TOK:TOK + 1].bitcast(I32))
                e = dve.value_load(tab[0:1, 0, bass.ds(blk(i, u), 1)], min_val=0, max_val=E - 1)
                V.tensor_copy(gt[:, u % U:u % U + 1], xb[:, u % 2, bass.ds(e + GATE, 1)]).then_inc(s_meta, 1)

            def gate(i, u):
                dve.wait_ge(s_y, n(i, u))
                dve.wait_ge(s_meta, n(i, u))
                if real(i, u - 2):
                    dve.wait_ge(s_add, i * (U * 16) + (u - 2 + 1) * 16)
                V.tensor_scalar(yg[:, u % 2, :], bank[6 + u % 2][:, 0:D], gt[:, u % U:u % U + 1], None, ALU.mult).then_inc(s_yg, 1)

            def slot(i, u):
                if real(i, u + 1):
                    x_lo(i, u + 1)
                dve.wait_ge(s_g, n(i, u))
                dve.wait_ge(s_sa, n(i, u))
                if real(i, u - 1):
                    dve.wait_ge(s_at, n(i, u - 1))
                V.tensor_tensor(ac[:], bank[2 * (u % 2) + 1][:, :], sa[:], ALU.mult).then_inc(s_ac, 1)
                if real(i, u - 1):
                    gate(i, u - 1)

            turns(dve, lambda: x_lo(0, 0), slot, lambda i: gate(i, -1))

        @block.gpsimd
        def _(pool):
            def slot(i, u):
                pool.wait_ge(s_yg, n(i, u))
                if real(i, u - 1):
                    pool.wait_ge(s_add, i * (U * 16) + u * 16)
                pool.sem_inc(s_turn, 1)
                nc.gpsimd.indirect_dma_start(out=out[:, :],
                                             out_offset=bass.IndirectOffsetOnAxis(ap=tk[:, u:u + 1], axis=0),
                                             in_=yg[:, u % 2, :], in_offset=None, compute_op=ALU.add).then_inc(s_add, 16)

            turns(pool, lambda: None, slot, lambda i: None)
            pool.wait_ge(s_add, 16 * NT)


_INS = ["x", "ctx_1024", "L0_xattn_W_q", "L0_xattn_W_k", "L0_xattn_W_v", "L0_xattn_W_out", "L0_xattn_b_q", "L0_xattn_b_k",
        "L0_xattn_b_v", "L0_xattn_b_out", "L0_ffn_W1", "L0_ffn_b1", "L0_ffn_W2", "L0_ffn_b2", "L0_ffn_Wr", "L0_ffn_br"]
_TRANSPOSED = ("L0_xattn_W_q", "L0_xattn_W_k", "L0_xattn_W_v", "L0_xattn_W_out")


def shape_constants(NB):
    import numpy as np
    T, REG, NBLK = sizes(NB)
    c = np.zeros((P, C_END), np.float32)
    r = np.arange(P)
    c[:, C_ID:C_ID + P] = np.eye(P)
    c[:, C_TRI:C_TRI + P] = r[:, None] < r[None, :]
    c[:, C_ONE:C_ONE + P] = 1
    c[:, C_I8:C_I8 + E] = np.arange(E)
    c[:, C_BASE:C_BASE + E] = np.arange(E) * REG
    c[:, C_THR:C_THR + NB] = np.arange(NB) * P
    c[:, C_BLK:C_BLK + 144] = np.arange(144)
    e = np.arange(E)
    c[:, C_T8:C_T8 + E * E] = (e[None, :] <= e[:, None]).reshape(-1)
    c[:, C_P] = r
    return c


def kernel(**inputs):
    import numpy as _np
    import concourse.bacc as _bacc
    from concourse.bass_utils import run_bass_kernel_spmd as _run

    nc = _bacc.Bacc("TRN2", target_bir_lowering=False, num_devices=1)
    arrays, args = {}, []
    NB = inputs["x"].shape[0]
    laid = {n: _np.ascontiguousarray(_np.asarray(inputs[n]).T if n in _TRANSPOSED else inputs[n]) for n in _INS}
    laid["constants"] = shape_constants(NB)
    for name, a in laid.items():
        arrays[f"in_{name}"] = a
        args.append(nc.dram_tensor(f"in_{name}", a.shape, mybir.dt.from_np(a.dtype), kind="ExternalInput").ap())
    args.append(nc.dram_tensor("out_rows", (NB * P + P, D), F32, kind="ExternalOutput").ap())
    moe_layer(nc, *args)
    r = _run(nc, [arrays], core_ids=[0])
    return r.results[0]["out_rows"][:NB * P].reshape(NB, P, D)
```

```python
from contextlib import ExitStack

import concourse.bass as bass
from concourse import mybir

F32 = mybir.dt.float32
F32R = mybir.dt.float32r
BF16 = mybir.dt.bfloat16
I32 = mybir.dt.int32
U32 = mybir.dt.uint32
ALU = mybir.AluOpType
ACT = mybir.ActivationFunctionType
AX_X = mybir.AxisListType.X

P = 128
D = 256
KC = D // P
H = 16
DH = D // H
E = 8
TOPK = 2
F = 512
FC = F // P
EPS = 1e-5
SCALE = DH ** -0.5

GB = 4
LB = 8
HC = 4
NCH = H // HC
TERMS_Q = (0, 0, 1, 1, 0, 2)
TERMS_K = (0, 1, 0, 1, 2, 0)
SCG = 16 * GB * TOPK
NSTK = 2 * len(TERMS_Q)
KS = len(TERMS_Q) * DH
ROW = 272
TOK, GATE = D, D + 1

C_ID, C_TRI, C_ONE, C_I8, C_BASE, C_THR, C_BLK, C_T8, C_P, C_END = 0, 128, 256, 384, 392, 400, 464, 608, 672, 673


def sizes(NB):
    T = NB * P
    REG = T + P
    NBLK = (T * TOPK + E * (P - 1)) // P
    return T, REG, NBLK


def moe_layer(nc, x, ctx_in, wqT, wkT, wvT, woT, bq, bk, bv, bo, w1, b1, w2, b2, wr, br, cst, out):
    NB = x.shape[0]
    T, REG, NBLK = sizes(NB)
    NI = NB // LB
    assert NB % LB == 0 and NI >= 3

    xs = nc.dram_tensor("routed_rows", (E * REG + P, ROW), F32, kind="Internal").ap()
    assert NB // GB == E * KC
    w1p = [nc.dram_tensor(f"w1_{n}_dram", (E * D, 2 * F), F32, kind="Internal").ap() for n in ("hi", "lo")]

    outer = ExitStack()
    with outer:
        def sem(name):
            return outer.enter_context(nc.semaphore(name))

        bank = [outer.enter_context(nc.psum_tensor(f"bank{i}", [P, 512], F32)) for i in range(8)]
        consts = outer.enter_context(nc.sbuf_tensor("consts", [P, C_END], F32))
        cm = outer.enter_context(nc.sbuf_tensor("routed_before", [P, GB + 1, E], BF16))
        ones_bf = outer.enter_context(nc.sbuf_tensor("ones_bf", [P, P], BF16))
        s_const = sem("const_loaded")
        s_carry = sem("carry_added")
        ident = consts[:, C_ID:C_ID + P]

        attention(nc, sem, bank, consts, ident, ones_bf, cm, s_const, s_carry, NB, NI, REG, xs,
                  x, ctx_in, wqT, wkT, wvT, woT, bq, bk, bv, bo, wr, br, w1, w1p, cst, out)
        experts(nc, sem, bank, consts, ident, ones_bf, cm, T, REG, NBLK, xs, w1p, b1, w2, b2, out)


def attention(nc, sem, bank, consts, ident, ones_bf, cm, s_const, s_carry, NB, NI, REG, xs,
              x, ctx_in, wqT, wkT, wvT, woT, bq, bk, bv, bo, wr, br, w1, w1p, cst, out):
    parts_dram = nc.dram_tensor("qk_parts_dram", (2, 3, KC, P, GB * P), BF16, kind="Internal").ap()

    def real(i, j):
        return not isinstance(i, int) or 0 <= LB * i + j < NB

    def count(i, j, per=1, done=None):
        return i * (LB * per) + (j * per + (per if done is None else done))

    def groups(i, j, per=1):
        return i * (LB // GB * per) + (j // GB + 1) * per

    def batch(i, j):
        return i * LB + j

    def group(i, j):
        return i * (LB // GB) + j // GB

    with ExitStack() as ctx:
        def sb(name, shape, dt):
            return ctx.enter_context(nc.sbuf_tensor(name, shape, dt))

        w_in = sb("w_in", [P, 4, KC, D], F32)
        w1c, w1ch = (w_in[:, k:k + 2].rearrange("p a c n -> p (a c n)") for k in (0, 2))
        w_hi = sb("w_hi", [P, 4, KC, D], F32R)
        w_lo = sb("w_lo", [P, 4, KC, D], F32R)
        bqk = sb("bqk", [P, 4], F32)
        bvc = sb("bv", [P, KC], F32)
        bob = sb("bo_rows", [P, D], F32)
        brb = sb("br_rows", [P, E], F32)
        wrs = sb("wr_sb", [P, KC, E], F32)
        tri_bf = sb("tri_bf", [P, P], BF16)
        id_bf = sb("id_bf", [P, P], BF16)
        mhalf = sb("minus_half", [P, 2], F32)
        zero = sb("zero", [P, 2], F32)

        x_in = sb("x_in", [P, GB, D], F32)
        c_in = sb("c_in", [P, GB, D], F32)
        xn = sb("xn", [P, GB, D], F32)
        st1 = sb("ln1_stats", [P, 2, 6], F32)
        mv1 = sb("ln1_mean_var", [P, 2, 2], F32)
        ve1 = sb("ln1_var_eps", [P, 2], F32)
        rs1 = sb("ln1_rstd", [P, 2], F32)
        nm1 = sb("ln1_minus_mean", [P, 2], F32)
        nb1 = sb("ln1_shift", [P, 2], F32)
        t_hi = sb("t_hi", [P, 4, GB * P], F32R)
        t_lo = sb("t_lo", [P, 4, GB * P], F32R)
        parts = sb("qk_parts", [P, 4, 3, GB * P], BF16)
        rem = sb("qk_rem", [P, 4, GB * P], F32)
        qst = [sb(f"q_stack{i}", [P, H, GB * P], BF16) for i in range(2)]
        kst = [sb(f"k_stack{i}", [P, H, GB * P], BF16) for i in range(2)]
        va = sb("v_ones", [P, LB, H, 32], F32)
        mx = sb("row_max", [P, 2, H], F32)
        nm = sb("minus_max", [P, 2, H], BF16)
        nmT = sb("minus_max_T", [2 * H, 2, P], BF16)
        pT = sb("probs_T", [P, NCH, 512], F32)
        cu = sb("ctx_sums_T", [P, NCH, P], F32)
        rs = sb("recip_sum", [P, H], F32)
        cn = sb("ctx_norm", [P, D], F32)
        ch = sb("ctxT_hi", [P, KC, P], F32R)
        cl = sb("ctxT_lo", [P, KC, P], F32R)
        xres = sb("x_res", [P, 2, D], F32)
        xrb = sb("x_res_bo", [P, 2, D], F32)
        x2 = sb("x2", [P, 2, D], F32)
        st2 = sb("ln2_stats", [P, 6], F32)
        mv2 = sb("ln2_mean_var", [P, 2, 2], F32)
        ve2 = sb("ln2_var_eps", [P, 1], F32)
        rs2 = sb("ln2_rstd", [P, 2], F32)
        nm2 = sb("ln2_minus_mean", [P, 2], F32)
        nb2 = sb("ln2_shift", [P, 2], F32)
        xr = sb("rows", [P, LB, ROW], F32)
        nT = sb("xn2_T", [P, KC, P], F32)
        lg = sb("logits", [P, LB, E], F32)
        mx8 = sb("top_vals", [P, GB, 8], F32)
        ix8 = sb("top_idx", [P, GB, 8], U32)
        ixf = sb("top_idx_f", [P, GB, TOPK], F32)
        oh = sb("onehot", [P, GB, TOPK, E], F32)
        mask = sb("mask", [P, GB, E], BF16)
        gd = sb("gate_diff", [P, GB], F32)
        ge = sb("gate_exp", [P, GB], F32)
        gden = sb("gate_den", [P, GB], F32)
        g12 = sb("gates", [P, GB, TOPK], F32)
        gg = sb("gates_oh", [P, GB, TOPK, E], F32)
        tpos = sb("rank_base", [P, GB, E], F32)
        dsel = sb("dest_sel", [P, GB, TOPK, E], F32)
        dstf = sb("dest_f", [P, GB, TOPK], F32)
        dsti = sb("dest_i", [P, 2, GB, TOPK], I32)
        tokf = sb("token_f", [P, LB], F32)

        s_w = sem("weights_loaded"); s_wh = sem("weights_hi"); s_wl = sem("weights_lo"); s_set = sem("setup_done"); s_bvr = sem("bv_columns"); s_bvo = sem("bv_projected"); s_bo = sem("bo_complete")
        s_ldx = [sem(f"x_loaded{i}") for i in range(GB)]
        s_ldc = [sem(f"ctx_loaded{i}") for i in range(GB)]
        s_ldr = [sem(f"xres_loaded{i}") for i in range(2)]
        s_st1 = sem("ln1_stats_done"); s_pr1 = sem("ln1_rstd_parts"); s_pr2 = sem("ln2_rstd_parts"); s_mv1 = sem("ln1_mv_done"); s_ve1 = sem("ln1_ve_done")
        s_rs1 = sem("ln1_rstd_done"); s_xn = sem("ln1_done")
        s_xT = sem("xT_done"); s_xh = sem("xT_hi_done"); s_xl = sem("xT_lo_done")
        s_qk = sem("qk_proj_done"); s_ev = sem("qk_copied"); s_p0 = sem("part0_done"); s_r = sem("rem_done"); s_p1 = sem("part1_done")
        s_p2 = sem("part2_done"); s_stk = sem("stacks_loaded"); s_prt = [sem(f"{w}_parts_stored") for w in "qk"]
        s_w1c = sem("w1_chunk_loaded"); s_w1h = sem("w1_chunk_hi"); s_w1l = sem("w1_chunk_lo"); s_w1s = sem("w1_parts_stored")
        s_vm = sem("v_proj_done"); s_v = sem("v_done")
        s_s = sem("scores_done"); s_mx = sem("max_done"); s_nmh = sem("max_hi_done"); s_nm = sem("minus_max_done")
        s_mt = sem("max_T_done"); s_mT = sem("max_T_copied"); s_mrow = [sem(f"max_rows_loaded{i}") for i in range(2)]
        s_st = sem("scoresT_done"); s_exp = sem("exp_done"); s_pv = sem("pv_done"); s_cu = sem("ctx_copied")
        s_t1 = sem("ctx_tok_done"); s_rs = sem("recip_done"); s_cn = sem("ctx_norm_done")
        s_t2 = sem("ctx_T_done"); s_ch = sem("ctx_hi_done"); s_cl = sem("ctx_lo_done"); s_out = sem("out_proj_done")
        s_xb = sem("xres_bo_done"); s_x2 = sem("x2_done"); s_x2d = [sem(f"x2_stored{i}") for i in range(2)]
        s_st2 = sem("ln2_stats_done"); s_mv2 = sem("ln2_mv_done"); s_ve2 = sem("ln2_ve_done")
        s_rs2 = sem("ln2_rstd_done"); s_n2 = sem("ln2_done")
        s_t3 = sem("xn2_T_done"); s_nT = sem("xn2_T_copied"); s_lg = sem("logits_done"); s_lgt = sem("logits_copied")
        s_top = sem("top_vals_done"); s_ix = sem("top_idx_done"); s_ixf = sem("top_idx_f_done"); s_oh = sem("onehot_done")
        s_mask = sem("mask_done"); s_gd = sem("gate_diff_done"); s_ge = sem("gate_exp_done")
        s_gden = sem("gate_den_done"); s_g1 = sem("gate1_done"); s_g2 = sem("gate2_done"); s_gg = sem("gates_oh_done")
        s_rk = sem("rank_done"); s_tp = sem("rank_read"); s_dsel = sem("dest_sel_done"); s_dstf = sem("dest_f_done")
        s_route = sem("routing_done"); s_zero = sem("v_zeroed"); s_ones = sem("ones_set"); s_sc = sem("rows_scattered"); s_free = sem("row_buffers_free")
        s_took = {"sp": sem("sp_waits_taken"), "dve": sem("dve_waits_taken"), "pool": sem("pool_waits_taken")}

        block = ctx.enter_context(nc.Block())

        def take(eng, name):
            eng.sem_inc(s_took[name], 1)

        def run(eng, slot, before):
            before()
            for j in range(LB):
                slot(0, j)
            with eng.Fori(1, NI - 1) as i:
                for j in range(LB):
                    slot(i, j)
            for j in range(LB):
                slot(NI - 1, j)
            for j in range(GB + 1):
                slot(NI, j)

        PROJ = {1: (("qk", 0), ("v", 0), ("qk", 1), ("v", 1)), 2: (("qk", 2), ("qk", 3), ("v", 2), ("v", 3))}

        def ahead(i, j, point, qk, v, xt):
            q, g1 = j % GB, (j // GB + 1) * GB
            if q in PROJ and real(i, g1):
                kind, n = PROJ[q][point]
                if kind == "qk":
                    qk(i, g1, n)
                else:
                    v(i, g1 + n)
            if q == 3 and point % 2 == 0 and real(i, g1 + GB):
                xt(i, g1 + GB + point // 2)
            if q == 0 and point % 2 == 0 and real(i, g1):
                xt(i, g1 + 2 + point // 2)

        def first_group(qk, v):
            for q in (1, 2):
                for kind, n in PROJ[q]:
                    if kind == "qk":
                        qk(0, 0, n)
                    else:
                        v(0, n)

        @block.sync
        def _(sp):
            def load_x(i, j):
                q = j % GB
                if real(i, j - GB):
                    sp.wait_ge(s_xn, groups(i, j - GB, 2) - (1 if q < 2 else 0))
                sp.dma_start(x_in[:, q, :], x[batch(i, j)]).then_inc(s_ldx[q], 16)

            def load_c(i, j):
                q = j % GB
                if real(i, j - GB):
                    sp.wait_ge(s_xT, count(i, j - GB))
                sp.dma_start(c_in[:, q, :], ctx_in[batch(i, j)]).then_inc(s_ldc[q], 16)

            def store_parts(i, j, o):
                w, c = o // KC, o % KC
                sp.wait_ge(s_p0, groups(i, j, 4) - 3 + o)
                sp.dma_start(parts_dram[w, 0, c], parts[:, o, 0, :]).then_inc(s_prt[w], 16)
                sp.wait_ge(s_p2, groups(i, j, 4) - 3 + o)
                sp.dma_start(parts_dram[w, 1:3, c].rearrange("t p n -> p t n"), parts[:, o, 1:3, :]).then_inc(s_prt[w], 16)

            def load_stack(i, j, w):
                par = (j // GB) % 2
                if real(i, j - 2 * GB):
                    sp.wait_ge(s_st, count(i, j - 2 * GB + GB - 1, NCH))
                    take(sp, "sp")
                stack, terms = ((qst, TERMS_Q), (kst, TERMS_K))[w]
                sp.wait_ge(s_prt[w], groups(i, j, 16 * 2 * KC))
                for s, part in enumerate(terms):
                    sp.dma_start(stack[par][DH * s:DH * (s + 1), :, :],
                                 parts_dram[w, part].rearrange("c (h d) n -> d (c h) n", d=DH)).then_inc(s_stk, 16)

            def before():
                sp.dma_start(consts[:], cst).then_inc(s_const, 16)
                for n, w in enumerate((wqT, wkT, wvT, woT)):
                    sp.dma_start(w_in[:, n], w.rearrange("(c p) n -> p c n", p=P)).then_inc(s_w, 16)
                sp.dma_start(wrs[:], wr.rearrange("(c p) e -> p c e", p=P)).then_inc(s_w, 16)
                for n, b in enumerate((bq, bq, bk, bk)):
                    c = n % 2
                    sp.dma_start(bqk[:, n:n + 1], b[c * P:(c + 1) * P].rearrange("(p o) -> p o", o=1)).then_inc(s_w, 16)
                for c in range(KC):
                    sp.dma_start(bvc[:, c:c + 1], bv[c * P:(c + 1) * P].rearrange("(p o) -> p o", o=1)).then_inc(s_w, 16)
                for dst, b in ((bob, bo), (brb, br)):
                    sp.dma_start(dst[:], b.rearrange("(o n) -> o n", o=1).to_broadcast([P, b.shape[0]])).then_inc(s_w, 16)
                for q in range(2 * GB):
                    load_x(0, q)
                    load_c(0, q)
                for o in range(4):
                    store_parts(0, 0, o)
                for w in range(2):
                    load_stack(0, 0, w)

            def slot(i, j):
                q = j % GB
                if real(i, j - 1):
                    jj = j - 1
                    if real(i, jj - 2):
                        sp.wait_ge(s_xb, count(i, jj - 2))
                    sp.dma_start(xres[:, jj % 2, :], x[batch(i, jj)]).then_inc(s_ldr[jj % 2], 16)
                g0 = (j // GB) * GB
                for load, later in ((load_x, {0: range(4)}), (load_c, {0: range(2), 1: range(2, 4)})):
                    for b in later.get(q, ()):
                        if real(i, g0 + 2 * GB + b):
                            load(i, g0 + 2 * GB + b)
                if real(i, j - 3):
                    jj = j - 3
                    sp.wait_ge(s_x2, count(i, jj))
                    sp.dma_start(out[bass.ds(batch(i, jj) * P, P), :], x2[:, jj % 2, :]).then_inc(s_x2d[jj % 2], 16)
                g1 = (j // GB + 1) * GB
                if q == 1 and real(i, j):
                    sp.wait_ge(s_wl, 1)
                    if real(i, j - GB):
                        sp.wait_ge(s_w1s, groups(i, j - GB, 32))
                    sp.dma_start(w1c, w1.rearrange("e k n -> (e k) n")[bass.ds(group(i, j) * P, P), :]).then_inc(s_w1c, 16)
                if q == 0 and real(i, j - GB):
                    sp.wait_ge(s_w1l, groups(i, j - GB))
                    for part, src in enumerate((w1ch, w1c)):
                        sp.dma_start(w1p[part][bass.ds(group(i, j - GB) * P, P), :], src).then_inc(s_w1s, 16)
                if q == 1 and real(i, g1):
                    store_parts(i, g1, 0)
                if q == 2 and real(i, g1):
                    store_parts(i, g1, 2)
                if real(i, j):
                    sp.wait_ge(s_mT, count(i, j))
                    for part in range(2):
                        sp.dma_start(qst[(j // GB) % 2][KS + part:KS + part + 1, :, q * P:(q + 1) * P],
                                     nmT[H * part:H * (part + 1), j % 2, :]).then_inc(s_mrow[j % 2], 16)
                if q == 1 and real(i, g1):
                    store_parts(i, g1, 1)
                    load_stack(i, g1, 0)
                if q == 2 and real(i, g1):
                    store_parts(i, g1, 3)
                    load_stack(i, g1, 1)

            run(sp, slot, before)
            sp.wait_ge(s_x2d[0], 16 * (NB // 2))
            sp.wait_ge(s_x2d[1], 16 * (NB // 2))
            sp.wait_ge(s_w1s, 32 * (NB // GB))

        @block.tensor
        def _(pe):
            mm = nc.tensor.matmul

            def split3(dst, a_hi, a_lo, b_hi, b_lo):
                n = len(a_hi)
                for c in range(n):
                    mm(dst, a_hi[c], b_hi[c], start=(c == 0), stop=False)
                    mm(dst, a_hi[c], b_lo[c], start=False, stop=False)
                    last = mm(dst, a_lo[c], b_hi[c], start=False, stop=(c == n - 1))
                return last

            def to_T(i, j):
                q = j % GB
                if q % 2 == 0:
                    pe.wait_ge(s_xn, groups(i, j, 2) - (1 if q == 0 else 0))
                pe.wait_ge(s_ldc[q], groups(i, j, 16))
                if q == 0:
                    if real(i, j - 1):
                        pe.wait_ge(s_v, count(i, j - 1))
                else:
                    pe.wait_ge(s_xl, count(i, j - 1))
                for c in range(2 * KC):
                    src = (xn if c < KC else c_in)[:, q, (c % KC) * P:(c % KC + 1) * P]
                    last = nc.tensor.transpose(bank[5][:, c * P:(c + 1) * P], src, ident)
                last.then_inc(s_xT, 1)

            def qk_proj(i, j, o):
                if o == 0:
                    pe.wait_ge(s_xl, count(i, j + GB - 1))
                elif o < 3:
                    pe.wait_ge(s_v, count(i, j + o - 1))
                else:
                    pe.wait_ge(s_ev, groups(i, j, 4) - 4 + o)
                w, c0, src = (0 if o < 2 else 1), (o % 2) * P, (0 if o < 2 else KC)
                split3(bank[5][:, :],
                       [w_hi[:, w, c, c0:c0 + P] for c in range(KC)], [w_lo[:, w, c, c0:c0 + P] for c in range(KC)],
                       [t_hi[:, src + c, :] for c in range(KC)], [t_lo[:, src + c, :] for c in range(KC)]
                       ).then_inc(s_qk, 1)

            def v_proj(i, j):
                q = j % GB
                if q < 3:
                    pe.wait_ge(s_ev, groups(i, j, 4) - (3, 2, 0)[q])
                else:
                    pe.wait_ge(s_v, count(i, j - 1))
                sl = slice(q * P, (q + 1) * P)
                split3(bank[5][:, 0:D],
                       [t_hi[:, KC + c, sl] for c in range(KC)], [t_lo[:, KC + c, sl] for c in range(KC)],
                       [w_hi[:, 2, c, :] for c in range(KC)], [w_lo[:, 2, c, :] for c in range(KC)]
                       ).then_inc(s_vm, 1)

            def scores(i, j, c):
                par, sl = (j // GB) % 2, slice((j % GB) * P, (j % GB + 1) * P)
                if c == 0 and j % GB == 0:
                    pe.wait_ge(s_stk, groups(i, j, 16 * NSTK))
                if c >= 2 or real(i, j - 1):
                    pe.wait_ge(s_mx, count(i, j, NCH, c - 1))
                for r in range(HC):
                    h = HC * c + r
                    last = mm(bank[c % 2][:, r * P:(r + 1) * P], qst[par][0:KS, h, sl], kst[par][0:KS, h, sl],
                              start=True, stop=True)
                last.then_inc(s_s, 1)

            def scores_T(i, j, c):
                par, sl = (j // GB) % 2, slice((j % GB) * P, (j % GB + 1) * P)
                if c == 0:
                    pe.wait_ge(s_mrow[j % 2], i * (LB // 2 * 32) + (j // 2 + 1) * 32)
                if c >= 2 or real(i, j - 1):
                    pe.wait_ge(s_exp, count(i, j, NCH, c - 1))
                for r in range(HC):
                    h = HC * c + r
                    last = mm(bank[2 + c % 2][:, r * P:(r + 1) * P], kst[par][0:KS + 2, h, sl],
                              qst[par][0:KS + 2, h, sl], start=True, stop=True)
                last.then_inc(s_st, 1)

            def pv(i, j, c):
                pe.wait_ge(s_exp, count(i, j, NCH, c + 1))
                if c == 0:
                    pe.wait_ge(s_v, count(i, j))
                    if real(i, j - 1):
                        pe.wait_ge(s_cu, count(i, j - 1))
                for r in range(HC):
                    last = mm(bank[4][32 * r:32 * r + 32, c * P:(c + 1) * P], va[:, j % LB, HC * c + r, :],
                              pT[:, c, r * P:(r + 1) * P], start=True, stop=True)
                last.then_inc(s_pv, 1)

            def bank6_read(i, j, *readers):
                for s, lag in readers:
                    if real(i, j - lag):
                        pe.wait_ge(s, count(i, j - lag))
                        break

            def before():
                pe.wait_ge(s_const, 16)
                pe.wait_ge(s_wl, 1)
                pe.wait_ge(s_set, 1)
                pe.wait_ge(s_bvr, 1)
                for c in range(KC):
                    last = mm(bank[7][:, 0:D], cn[:, c * P:(c + 1) * P], w_in[:, 3, c, :], start=(c == 0), stop=(c == KC - 1))
                last.then_inc(s_bvo, 1)
                for q in range(GB):
                    to_T(0, q)
                first_group(qk_proj, v_proj)
                for q in range(2):
                    to_T(0, GB + q)
                pe.wait_ge(s_bo, 1)
                pe.wait_ge(s_ones, 3)

            def slot(i, j):
                q = j % GB
                if real(i, j):
                    scores(i, j, 0)
                    scores(i, j, 1)
                if real(i, j - 3):
                    pe.wait_ge(s_cl, count(i, j - 3))
                    split3(bank[7][:, 0:D], [ch[:, c, :] for c in range(KC)], [cl[:, c, :] for c in range(KC)],
                           [w_hi[:, 3, c, :] for c in range(KC)], [w_lo[:, 3, c, :] for c in range(KC)]
                           ).then_inc(s_out, 1)
                if real(i, j - 2):
                    pe.wait_ge(s_cu, count(i, j - 2))
                    bank6_read(i, j, (s_lgt, 4), (s_mT, 1))
                    for c in range(NCH):
                        last = nc.tensor.transpose(bank[6][:, c * P:(c + 1) * P], cu[:, c, :], ident)
                    last.then_inc(s_t1, 1)
                if real(i, j - 1):
                    scores_T(i, j - 1, 0)
                    scores_T(i, j - 1, 1)
                if real(i, j):
                    scores(i, j, 2)
                ahead(i, j, 0, qk_proj, v_proj, to_T)
                if real(i, j - 1):
                    pv(i, j - 1, 0)
                if real(i, j):
                    scores(i, j, 3)
                if real(i, j - 1):
                    scores_T(i, j - 1, 2)
                    pv(i, j - 1, 1)
                if q == 0 and real(i, j - 5):
                    pe.wait_ge(s_carry, groups(i, j - 5, GB + 1))
                    if real(i, j - 3):
                        pe.wait_ge(s_x2, count(i, j - 3))
                    mm(bank[7][:, 0:GB * E], tri_bf[:], mask[:].rearrange("p b e -> p (b e)"), start=True, stop=False)
                    mm(bank[7][:, 0:GB * E], ones_bf[:], cm[:, 0:GB, :].rearrange("p b e -> p (b e)"),
                       start=False, stop=True).then_inc(s_rk, 1)
                if real(i, j - 2):
                    pe.wait_ge(s_cn, count(i, j - 2))
                    if real(i, j - 3):
                        pe.wait_ge(s_x2, count(i, j - 3))
                    if q == 0 and real(i, j - 5):
                        pe.wait_ge(s_tp, groups(i, j - 5))
                    for c in range(KC):
                        last = nc.tensor.transpose(bank[7][:, c * P:(c + 1) * P], cn[:, c * P:(c + 1) * P], ident)
                    last.then_inc(s_t2, 1)
                ahead(i, j, 1, qk_proj, v_proj, to_T)
                if real(i, j - 1):
                    scores_T(i, j - 1, 3)
                    pv(i, j - 1, 2)
                if real(i, j):
                    pe.wait_ge(s_nm, count(i, j))
                    bank6_read(i, j, (s_cn, 2), (s_lgt, 4), (s_mT, 1))
                    nc.tensor.transpose(bank[6][0:2 * H, 0:P // 2].bitcast(BF16),
                                        nm[:].rearrange("p t h -> p (t h)"), id_bf[:]).then_inc(s_mt, 1)
                ahead(i, j, 2, qk_proj, v_proj, to_T)
                if real(i, j - 3):
                    pe.wait_ge(s_n2, count(i, j - 3))
                    bank6_read(i, j, (s_mT, 0), (s_cn, 2), (s_lgt, 4))
                    for c in range(KC):
                        last = nc.tensor.transpose(bank[6][:, c * P:(c + 1) * P],
                                                   xr[:, (j - 3) % LB, c * P:(c + 1) * P], ident)
                    last.then_inc(s_t3, 1)
                if real(i, j - 1):
                    pv(i, j - 1, 3)
                if real(i, j - 3):
                    pe.wait_ge(s_nT, count(i, j - 3))
                    for c in range(KC):
                        last = mm(bank[6][:, 0:E], nT[:, c, :], wrs[:, c, :], start=(c == 0), stop=(c == KC - 1))
                    last.then_inc(s_lg, 1)
                ahead(i, j, 3, qk_proj, v_proj, to_T)

            run(pe, slot, before)

        @block.scalar
        def _(act):
            def xT_hi(i, j):
                q = j % GB
                act.wait_ge(s_xT, count(i, j))
                if q == 0 and real(i, j - 1):
                    act.wait_ge(s_vm, count(i, j - 1))
                nc.scalar.activation(t_hi[:, :, q * P:(q + 1) * P],
                                     bank[5][:, :].rearrange("p (c n) -> p c n", c=4), ACT.Copy).then_inc(s_xh, 1)

            def qk_out(i, j, o):
                if o == 0 and real(i, j - GB):
                    act.wait_ge(s_p2, groups(i, j - GB, 4))
                act.wait_ge(s_qk, groups(i, j, 4) - 3 + o)
                nc.scalar.activation(rem[:, o, :], bank[5][:, :], ACT.Identity, bias=bqk[:, o:o + 1]).then_inc(s_ev, 1)

            def part1(i, j, o):
                act.wait_ge(s_r, groups(i, j, 4) - 3 + o)
                nc.scalar.activation(parts[:, o, 1, :], rem[:, o, :], ACT.Copy).then_inc(s_p1, 1)

            def v_rows(i, j):
                act.wait_ge(s_vm, count(i, j))
                if real(i, j - LB):
                    act.wait_ge(s_pv, count(i, j - LB, NCH))
                nc.scalar.activation(va[:, j % LB, :, 0:DH], bank[5][:, 0:D].rearrange("p (h d) -> p h d", h=H),
                                     ACT.Copy).then_inc(s_v, 1)

            def ln1_norm(i, j):
                act.wait_ge(s_rs1, groups(i, j, 2) - (1 if j % GB == 0 else 0))
                for h in range(2):
                    if real(i, j + h - GB):
                        act.wait_ge(s_xT, count(i, j + h - GB))
                    last = nc.scalar.activation(xn[:, j % GB + h, :], x_in[:, j % GB + h, :], ACT.Identity,
                                                bias=nb1[:, h:h + 1], scale=rs1[:, h:h + 1])
                last.then_inc(s_xn, 1)

            def exps(i, j, c):
                act.wait_ge(s_st, count(i, j, NCH, c + 1))
                if real(i, j - 1):
                    act.wait_ge(s_pv, count(i, j - 1, NCH, c + 1))
                nc.scalar.activation(pT[:, c, :], bank[2 + c % 2][:, :], ACT.Exp, scale=SCALE).then_inc(s_exp, 1)

            def before():
                act.wait_ge(s_w, 16 * 13)
                nc.scalar.activation(w_hi[:].rearrange("p a b c -> p (a b c)"), w_in[:].rearrange("p a b c -> p (a b c)"),
                                     ACT.Copy).then_inc(s_wh, 1)
                for h in range(2):
                    ln1_norm(0, 2 * h)
                for q in range(GB):
                    xT_hi(0, q)
                act.wait_ge(s_zero, 1)
                for h in range(2, 4):
                    ln1_norm(0, 2 * h)
                first_group(lambda i, j, o: (qk_out(i, j, o), part1(i, j, o)), v_rows)
                for q in range(2):
                    xT_hi(0, GB + q)

            def slot(i, j):
                q, g1 = j % GB, (j // GB + 1) * GB
                if real(i, j - 1):
                    exps(i, j - 1, 0)
                    exps(i, j - 1, 1)
                ahead(i, j, 0, qk_out, v_rows, xT_hi)
                if real(i, j - 1):
                    exps(i, j - 1, 2)
                if real(i, j - 3):
                    jj = j - 3
                    act.wait_ge(s_rs2, count(i, jj))
                    if real(i, jj - LB):
                        act.wait_ge(s_free, count(i, jj - LB) + LB)
                    nc.scalar.activation(xr[:, jj % LB, 0:D], x2[:, jj % 2, :], ACT.Identity,
                                         bias=nb2[:, jj % 2:jj % 2 + 1], scale=rs2[:, jj % 2:jj % 2 + 1]).then_inc(s_n2, 1)
                if q == 3 and real(i, j):
                    act.wait_ge(s_w1c, groups(i, j, 16))
                    nc.scalar.activation(w1ch.bitcast(F32R), w1c, ACT.Copy).then_inc(s_w1h, 1)
                if real(i, j - 2):
                    act.wait_ge(s_t2, count(i, j - 2))
                    if real(i, j - 3):
                        act.wait_ge(s_out, count(i, j - 3))
                    nc.scalar.activation(ch[:].rearrange("p c n -> p (c n)"), bank[7][:, 0:D], ACT.Copy).then_inc(s_ch, 1)
                ahead(i, j, 1, qk_out, v_rows, xT_hi)
                if q == 1 and real(i, g1):
                    part1(i, g1, 0)
                if q == 2 and real(i, g1):
                    part1(i, g1, 2)
                if real(i, j - 1):
                    exps(i, j - 1, 3)
                if real(i, j):
                    act.wait_ge(s_mt, count(i, j))
                    if real(i, j - 2):
                        act.wait_ge(s_mrow[j % 2], i * (LB // 2 * 32) + (j // 2) * 32)
                    nc.scalar.activation(nmT[:, j % 2, :], bank[6][0:2 * H, 0:P // 2].bitcast(BF16),
                                         ACT.Copy).then_inc(s_mT, 1)
                ahead(i, j, 2, qk_out, v_rows, xT_hi)
                if real(i, j - 3):
                    act.wait_ge(s_t3, count(i, j - 3))
                    if real(i, j - 4):
                        act.wait_ge(s_lg, count(i, j - 4))
                    nc.scalar.activation(nT[:].rearrange("p c n -> p (c n)"), bank[6][:, 0:D], ACT.Copy).then_inc(s_nT, 1)
                if real(i, j - 1):
                    act.wait_ge(s_pv, count(i, j - 1, NCH))
                    if real(i, j - 2):
                        act.wait_ge(s_t1, count(i, j - 2))
                    nc.scalar.activation(cu[:].rearrange("p c n -> p (c n)"), bank[4][:, :], ACT.Copy).then_inc(s_cu, 1)
                if q == 2 and real(i, g1):
                    part1(i, g1, 3)
                if q == 1 and real(i, g1):
                    part1(i, g1, 1)
                if q == 3 and real(i, j - 4):
                    act.wait_ge(s_gd, groups(i, j - 4))
                    nc.scalar.activation(ge[:], gd[:], ACT.Exp).then_inc(s_ge, 1)
                ahead(i, j, 3, qk_out, v_rows, xT_hi)
                if q in (1, 2) and real(i, g1 + GB):
                    ln1_norm(i, g1 + GB + 2 * (q - 1))

            run(act, slot, before)

        @block.vector
        def _(dve):
            V = nc.vector

            def ln1_stats(i, j):
                n = groups(i, j, 2) - (1 if j % GB == 0 else 0)
                for h in range(2):
                    dve.wait_ge(s_ldx[j % GB + h], groups(i, j, 16))
                    V.bn_stats(st1[:, h, :], x_in[:, j % GB + h, :]).then_inc(s_st1, 1)
                dve.wait_ge(s_st1, 2 * n)
                if real(i, j - 2):
                    dve.wait_ge(s_rs1, n - 1)
                take(dve, "dve")
                for h in range(2):
                    V.bn_aggr(mv1[:, h, :], st1[:, h, :]).then_inc(s_mv1, 1)
                dve.wait_ge(s_mv1, 2 * n)
                V.tensor_scalar(ve1[:], mv1[:, :, 1], EPS, None, ALU.add).then_inc(s_ve1, 1)

            def xT_lo(i, j):
                q = j % GB
                dve.wait_ge(s_xh, count(i, j))
                V.tensor_tensor(t_lo[:, :, q * P:(q + 1) * P], bank[5][:, :].rearrange("p (c n) -> p c n", c=4),
                                t_hi[:, :, q * P:(q + 1) * P].bitcast(F32), ALU.subtract).then_inc(s_xl, 1)

            def remainder(i, j, o):
                n = groups(i, j, 4) - 3 + o
                if o == 0 and real(i, j - GB):
                    dve.wait_ge(s_prt[1], groups(i, j - GB, 16 * 2 * KC))
                dve.wait_ge(s_ev, n)
                V.tensor_copy(parts[:, o, 0, :], rem[:, o, :]).then_inc(s_p0, 1)
                dve.wait_ge(s_p0, n)
                V.tensor_tensor(rem[:, o, :], rem[:, o, :], parts[:, o, 0, :], ALU.subtract).then_inc(s_r, 1)

            def maxima(i, j, c):
                dve.wait_ge(s_s, count(i, j, NCH, c + 1))
                V.tensor_reduce(mx[:, j % 2, HC * c:HC * (c + 1)], bank[c % 2][:, :].rearrange("p (h k) -> p h k", h=HC),
                                AX_X, ALU.max).then_inc(s_mx, 1)

            def top2(i, j):
                n, b0 = groups(i, j), j % LB
                dve.wait_ge(s_lgt, count(i, j + GB - 1))
                take(dve, "dve")
                for q in range(GB):
                    V.max(mx8[:, q, :], lg[:, b0 + q, :]).then_inc(s_top, 1)
                dve.wait_ge(s_top, n * GB)
                take(dve, "dve")
                for q in range(GB):
                    V.max_index(ix8[:, q, :], mx8[:, q, :], lg[:, b0 + q, :]).then_inc(s_ix, 1)
                V.tensor_tensor(gd[:], mx8[:, :, 1], mx8[:, :, 0], ALU.subtract).then_inc(s_gd, 1)

            def onehots(i, j):
                n = groups(i, j)
                dve.wait_ge(s_ix, n * GB)
                V.tensor_copy(ixf[:], ix8[:, :, 0:TOPK]).then_inc(s_ixf, 1)
                dve.wait_ge(s_ixf, n)
                for k in range(TOPK):
                    last = V.tensor_tensor(oh[:, :, k, :], ixf[:, :, k:k + 1].to_broadcast([P, GB, E]),
                                           consts[:, C_I8:C_I8 + E].rearrange("p (o e) -> p o e", o=1).to_broadcast([P, GB, E]),
                                           ALU.is_equal)
                last.then_inc(s_oh, 1)
                dve.wait_ge(s_oh, n)
                V.tensor_tensor(mask[:], oh[:, :, 0, :], oh[:, :, 1, :], ALU.add).then_inc(s_mask, 1)

            def carry(i, j, q):
                if q == 0:
                    dve.wait_ge(s_mask, groups(i, j))
                    V.tensor_copy(cm[:, 0, :], cm[:, GB, :]).then_inc(s_carry, 1)
                dve.wait_ge(s_carry, groups(i, j, GB + 1) - (GB - q))
                V.tensor_tensor(cm[:, q + 1, :], cm[:, q, :], mask[:, q, :], ALU.add).then_inc(s_carry, 1)

            def gates(i, j, step):
                n = groups(i, j)
                if step == 0:
                    dve.wait_ge(s_ge, n)
                    V.tensor_scalar(gden[:], ge[:], 1.0, None, ALU.add).then_inc(s_gden, 1)
                if step == 1:
                    dve.wait_ge(s_gden, n)
                    V.reciprocal(g12[:, :, 0], gden[:]).then_inc(s_g1, 1)
                if step == 2:
                    dve.wait_ge(s_g1, n)
                    V.tensor_tensor(g12[:, :, 1], g12[:, :, 0], ge[:], ALU.mult).then_inc(s_g2, 1)
                if step == 3:
                    dve.wait_ge(s_g2, n)
                    for k in range(TOPK):
                        V.tensor_tensor(gg[:, :, k, :], oh[:, :, k, :], g12[:, :, k:k + 1].to_broadcast([P, GB, E]),
                                        ALU.mult).then_inc(s_gg, 1)

            def ranks(i, j):
                dve.wait_ge(s_rk, groups(i, j))
                V.tensor_tensor(tpos[:], bank[7][:, 0:GB * E].rearrange("p (b e) -> p b e", b=GB),
                                consts[:, C_BASE:C_BASE + E].rearrange("p (o e) -> p o e", o=1).to_broadcast([P, GB, E]),
                                ALU.add).then_inc(s_tp, 1)

            def dests(i, j):
                n = groups(i, j)
                dve.wait_ge(s_tp, n)
                for k in range(TOPK):
                    V.tensor_tensor(dsel[:, :, k, :], oh[:, :, k, :], tpos[:], ALU.mult).then_inc(s_dsel, 1)

            def dest_sums(i, j):
                n = groups(i, j)
                dve.wait_ge(s_dsel, TOPK * n)
                V.tensor_reduce(dstf[:], dsel[:], AX_X, ALU.add).then_inc(s_dstf, 1)

            def row_ends(i, j):
                n = groups(i, j)
                b0, par = j % LB, (j // GB) % 2
                dve.wait_ge(s_dstf, n)
                if real(i, j - 2 * GB):
                    dve.wait_ge(s_free, count(i, j - 2 * GB + GB - 1) + LB)
                V.tensor_copy(dsti[:, par], dstf[:])
                dve.wait_ge(s_gg, TOPK * n)
                V.tensor_tensor(xr[:, b0:b0 + GB, GATE:GATE + E], gg[:, :, 0, :], gg[:, :, 1, :], ALU.add)
                V.tensor_copy(xr[:, b0:b0 + GB, TOK].bitcast(I32), tokf[:, b0:b0 + GB]).then_inc(s_route, 1)
                V.tensor_scalar(tokf[:, b0:b0 + GB], tokf[:, b0:b0 + GB], float(LB * P), None, ALU.add)

            def routing(i, j, point):
                q, g0 = j % GB, (j // GB) * GB
                if q == 3 and real(i, g0 - GB):
                    g = g0 - GB
                    if point == 1:
                        top2(i, g)
                    if point == 2:
                        onehots(i, g)
                    if point == 3:
                        carry(i, g, 0)
                        gates(i, g, 0)
                if q == 0 and real(i, j - 5):
                    g = g0 - 2 * GB
                    if point in ("max1", "cn", 0):
                        carry(i, g, {"max1": 1, "cn": 2, 0: 3}[point])
                    if point == "max3":
                        ranks(i, g)
                    if point == 1:
                        dests(i, g)
                        gates(i, g, 1)
                    if point == 2:
                        dest_sums(i, g)
                        gates(i, g, 2)
                    if point == 3:
                        gates(i, g, 3)
                        row_ends(i, g)

            def before():
                dve.sem_inc(s_free, LB)
                V.memset(mhalf[:], -0.5)
                V.memset(zero[:], 0.0)
                V.memset(cm[:, GB, :], 0.0)
                V.memset(ones_bf[:], 1.0)
                V.memset(xr[:, :, GATE + E:ROW], 0.0)
                dve.wait_ge(s_const, 16)
                V.tensor_copy(tri_bf[:], consts[:, C_TRI:C_TRI + P])
                V.tensor_copy(id_bf[:], ident)
                for b in range(LB):
                    last = V.tensor_scalar(tokf[:, b:b + 1], consts[:, C_P:C_P + 1], float(P * b), None, ALU.add)
                last.then_inc(s_set, 1)
                dve.wait_ge(s_w, 16 * 13)
                for c in range(KC):
                    last = V.tensor_copy(cn[:, c * P:(c + 1) * P], bvc[:, c:c + 1].to_broadcast([P, P]))
                last.then_inc(s_bvr, 1)
                dve.wait_ge(s_wh, 1)
                V.tensor_tensor(w_lo[:].rearrange("p a b c -> p (a b c)"), w_in[:].rearrange("p a b c -> p (a b c)"),
                                w_hi[:].rearrange("p a b c -> p (a b c)").bitcast(F32), ALU.subtract).then_inc(s_wl, 1)
                for h in range(2):
                    ln1_stats(0, 2 * h)
                for q in range(GB):
                    xT_lo(0, q)
                dve.wait_ge(s_bvo, 1)
                V.tensor_tensor(bob[:], bob[:], bank[7][:, 0:D], ALU.add).then_inc(s_bo, 1)
                for h in range(2, 4):
                    ln1_stats(0, 2 * h)
                first_group(remainder, lambda i, j: None)
                for q in range(2):
                    xT_lo(0, GB + q)

            def slot(i, j):
                q, g1 = j % GB, (j // GB + 1) * GB
                none = lambda i, j: None
                if real(i, j):
                    maxima(i, j, 0)
                jj = j - 3
                if real(i, jj):
                    dve.wait_ge(s_out, count(i, jj))
                    dve.wait_ge(s_xb, count(i, jj))
                    if real(i, jj - 2):
                        dve.wait_ge(s_n2, count(i, jj - 2))
                        dve.wait_ge(s_x2d[jj % 2], i * (LB // 2 * 16) + (jj - 2) // 2 * 16 + 16)
                    V.tensor_tensor(x2[:, jj % 2, :], bank[7][:, 0:D], xrb[:, jj % 2, :], ALU.add).then_inc(s_x2, 1)
                if real(i, j):
                    maxima(i, j, 1)
                if real(i, jj):
                    dve.wait_ge(s_x2, count(i, jj))
                    V.bn_stats(st2[:], x2[:, jj % 2, :]).then_inc(s_st2, 1)
                routing(i, j, "max1")
                psv = bank[6][:, :].rearrange("p (h d) -> p h d", h=H)
                if real(i, j - 2):
                    dve.wait_ge(s_t1, count(i, j - 2))
                    V.reciprocal(rs[:], psv[:, :, DH]).then_inc(s_rs, 1)
                if real(i, jj):
                    dve.wait_ge(s_st2, count(i, jj))
                    take(dve, "dve")
                    V.bn_aggr(mv2[:, jj % 2, :], st2[:]).then_inc(s_mv2, 1)
                if real(i, j - 2):
                    dve.wait_ge(s_rs, count(i, j - 2))
                    if real(i, j - 3):
                        dve.wait_ge(s_t2, count(i, j - 3))
                    V.tensor_tensor(cn[:].rearrange("p (h d) -> p h d", h=H), psv[:, :, 0:DH],
                                    rs[:].rearrange("p (h o) -> p h o", o=1).to_broadcast([P, H, DH]), ALU.mult).then_inc(s_cn, 1)
                if real(i, jj):
                    dve.wait_ge(s_mv2, count(i, jj))
                    if real(i, jj - 1):
                        dve.wait_ge(s_rs2, count(i, jj - 1))
                    V.tensor_scalar(ve2[:], mv2[:, jj % 2, 1:2], EPS, None, ALU.add).then_inc(s_ve2, 1)
                routing(i, j, "cn")
                if real(i, j):
                    maxima(i, j, 2)
                ahead(i, j, 0, remainder, none, xT_lo)
                routing(i, j, 0)
                if real(i, j):
                    maxima(i, j, 3)
                routing(i, j, "max3")
                if real(i, j):
                    dve.wait_ge(s_mx, count(i, j, NCH))
                    if real(i, j - 1):
                        dve.wait_ge(s_mt, count(i, j - 1))
                    V.tensor_scalar(nm[:, 0, :], mx[:, j % 2, :], -1.0, None, ALU.mult).then_inc(s_nmh, 1)
                    dve.wait_ge(s_nmh, count(i, j))
                    V.scalar_tensor_tensor(nm[:, 1, :], mx[:, j % 2, :], -1.0, nm[:, 0, :], ALU.mult,
                                           ALU.subtract).then_inc(s_nm, 1)
                if real(i, j - 2):
                    dve.wait_ge(s_ch, count(i, j - 2))
                    V.tensor_tensor(cl[:].rearrange("p c n -> p (c n)"), bank[7][:, 0:D],
                                    ch[:].rearrange("p c n -> p (c n)").bitcast(F32), ALU.subtract).then_inc(s_cl, 1)
                ahead(i, j, 1, remainder, none, xT_lo)
                routing(i, j, 1)
                ahead(i, j, 2, remainder, none, xT_lo)
                if real(i, j - 3):
                    dve.wait_ge(s_lg, count(i, j - 3))
                    V.tensor_tensor(lg[:, (j - 3) % LB, :], bank[6][:, 0:E], brb[:], ALU.add).then_inc(s_lgt, 1)
                if q == 3 and real(i, j):
                    dve.wait_ge(s_w1h, groups(i, j))
                    V.tensor_tensor(w1c.bitcast(F32R), w1c, w1ch, ALU.subtract).then_inc(s_w1l, 1)
                routing(i, j, 2)
                if q < 2 and real(i, g1 + GB):
                    ln1_stats(i, g1 + GB + 2 * q)
                ahead(i, j, 3, remainder, none, xT_lo)
                routing(i, j, 3)

            run(dve, slot, before)

        @block.gpsimd
        def _(pool):
            G = nc.gpsimd

            def part2(i, j, o):
                pool.wait_ge(s_p1, groups(i, j, 4) - 3 + o)
                G.tensor_tensor(parts[:, o, 2, :], rem[:, o, :], parts[:, o, 1, :], ALU.subtract).then_inc(s_p2, 1)

            def rstd(s_ve, s_pr, s_done, n, ve, mean, half, minus, rstd, shift):
                pool.wait_ge(s_ve, n)
                G.tensor_tensor(minus, zero[:, 0:half], mean, ALU.subtract).then_inc(s_pr, 1)
                G.tensor_tensor(rstd, ve, mhalf[:, 0:half], ALU.pow).then_inc(s_pr, 1)
                pool.wait_ge(s_pr, 2 * n)
                G.tensor_tensor(shift, minus, rstd, ALU.mult).then_inc(s_done, 1)

            def rstd1(i, j):
                n = groups(i, j, 2) - (1 if j % GB == 0 else 0)
                if real(i, j - 2):
                    pool.wait_ge(s_xn, n - 1)
                rstd(s_ve1, s_pr1, s_rs1, n, ve1[:], mv1[:, :, 0], 2, nm1[:], rs1[:], nb1[:])

            def free_rows(i, j):
                pool.wait_ge(s_sc, count(i, j, 16 * TOPK))
                pool.sem_inc(s_free, 1)

            def scatter(i, j):
                for k in range(TOPK):
                    G.indirect_dma_start(out=xs[:, :],
                                         out_offset=bass.IndirectOffsetOnAxis(
                                             ap=dsti[:, (j // GB) % 2, j % GB, k:k + 1], axis=0),
                                         in_=xr[:, j % LB, :], in_offset=None).then_inc(s_sc, 16)

            def before():
                G.memset(va[:].rearrange("p b h d -> p (b h d)"), 0.0).then_inc(s_zero, 1)
                pool.wait_ge(s_zero, 1)
                G.memset(va[:, :, :, DH:DH + 1], 1.0).then_inc(s_ones, 1)
                for k in range(2):
                    pool.wait_ge(s_ones, k + 1)
                    G.memset(kst[k][KS:KS + 2, :, :].rearrange("p h n -> p (h n)").bitcast(U32), 0x3F803F80).then_inc(s_ones, 1)
                pool.wait_ge(s_ones, 3)
                pool.wait_ge(s_set, 1)
                pool.wait_ge(s_w, 16 * 13)
                for h in range(4):
                    rstd1(0, 2 * h)
                for o in range(4):
                    part2(0, 0, o)
                pool.wait_ge(s_bo, 1)

            def slot(i, j):
                q, g1 = j % GB, (j // GB + 1) * GB
                if q in (1, 2) and real(i, g1 + GB):
                    rstd1(i, g1 + GB + 2 * (q - 1))
                if real(i, j - 2):
                    jj = j - 2
                    pool.wait_ge(s_ldr[jj % 2], i * (LB // 2 * 16) + (jj // 2 + 1) * 16)
                    if real(i, jj - 2):
                        pool.wait_ge(s_x2, count(i, jj - 2))
                    G.tensor_tensor(xrb[:, jj % 2, :], xres[:, jj % 2, :], bob[:], ALU.add).then_inc(s_xb, 1)
                if real(i, j - 3):
                    jj, k = j - 3, (j - 3) % 2
                    if real(i, jj - 2):
                        pool.wait_ge(s_n2, count(i, jj - 2))
                    rstd(s_ve2, s_pr2, s_rs2, count(i, jj), ve2[:], mv2[:, k, 0:1], 1, nm2[:, k:k + 1],
                         rs2[:, k:k + 1], nb2[:, k:k + 1])
                if j > 0 and real(i, j - 9):
                    free_rows(i, j - 9)
                if q == 1 and real(i, g1):
                    part2(i, g1, 0)
                if q == 2 and real(i, g1):
                    part2(i, g1, 2)
                    part2(i, g1, 3)
                if real(i, j - 8):
                    pool.wait_ge(s_route, groups(i, j - 8))
                    take(pool, "pool")
                    scatter(i, j - 8)
                    if j == LB - 1:
                        free_rows(i, j - 8)
                if q == 1 and real(i, g1):
                    part2(i, g1, 1)
                if isinstance(i, int) and i == NI and j == GB:
                    for b in range(1, GB):
                        scatter(i, j - 8 + b)

            run(pool, slot, before)
            pool.wait_ge(s_sc, 16 * TOPK * NB)


def experts(nc, sem, bank, consts, ident, ones_bf, cm, T, REG, NBLK, xs, w1p, b1, w2, b2, out):
    U = 4
    NT = (NBLK + U - 1) // U * U
    NTH = T // P
    NB1 = E * 2 * F
    with ExitStack() as ctx:
        def sb(name, shape, dt):
            return ctx.enter_context(nc.sbuf_tensor(name, shape, dt))

        w1h = sb("w1_hi", [P, E * KC * 2 * F], F32R)
        w1l = sb("w1_lo", [P, E * KC * 2 * F], F32R)
        w2s = sb("w2_sb", [P, E * FC * D], F32)
        bp = sb("bias_parts", [P, NB1 + E * D], BF16)
        scratch = sb("table_scratch", [P, (E + 2) * NT], F32)
        bsp = sb("bias_split", [P, NB1 // P + E * D // P], F32)
        bpt = sb("bias_part_tiles", [P, 3, NB1 // P + E * D // P], BF16)
        sel3 = sb("three_ones", [P, P], BF16)
        cnt = sb("counts", [P, E], F32)
        nbk = sb("blocks_of", [P, E], F32)
        incl = sb("blocks_upto", [P, E], F32)
        flat = scratch[0:1, :]
        ej, st = (flat[:, (E + k) * NT:(E + k + 1) * NT] for k in range(2))
        tab = sb("tables", [1, 2, NT], I32)
        prow = sb("idle_at", [1, E], I32)
        prf = sb("idle_at_f", [1, E], F32)
        xb = sb("block_rows", [P, 2, ROW], F32)
        tk = sb("block_tokens", [P, U], I32)
        gt = sb("block_gates", [P, U], F32)
        pad = xb[:, 1, :]
        xh = sb("block_T_hi", [P, 2, KC * P], F32R)
        xl = sb("block_T_lo", [P, 2, KC * P], F32R)
        sa = sb("silu_a", [P, F], F32)
        ac = sb("act", [P, F], F32)
        aT = sb("act_T", [P, FC, P], F32)
        yg = sb("y_gated", [P, 2, D], F32)

        s_cnt = sem("counts_summed"); s_t = sem("table_step"); s_tab = sem("tables_done")
        s_bl = sem("biases_loaded"); s_bs = sem("bias_step"); s_bd = sem("bias_parts_placed"); s_bz = sem("bias_zeroed")
        s_we = [sem(f"expert{e}_loaded") for e in range(E)]; s_ready = sem("experts_ready")
        s_pad = sem("idle_rows_ready"); s_pd = sem("idle_rows_stored")
        s_ld = [sem(f"block_loaded{k}") for k in range(2)]
        s_meta = sem("block_meta_read"); s_xT = sem("block_T_done"); s_xh = sem("block_hi_done"); s_xl = sem("block_lo_done")
        s_a = sem("w1a_done"); s_g = sem("w1g_done"); s_sa = sem("silu_done"); s_ac = sem("act_done")
        s_at = sem("act_T_done"); s_aT = sem("act_T_copied"); s_y = sem("w2_done"); s_yg = sem("y_gated_done")
        s_add = sem("rows_added"); s_turn = sem("add_turns")

        block = ctx.enter_context(nc.Block())

        def turns(eng, first, slot, last):
            first()
            for u in range(U):
                slot(0, u)
            with eng.Fori(1, NT // U - 1) as i:
                for u in range(U):
                    slot(i, u)
            for u in range(U):
                slot(NT // U - 1, u)
            last(NT // U)

        def blk(i, u):
            return i * U + u

        def real(i, u):
            return not isinstance(i, int) or 0 <= i * U + u < NT

        def n(i, u):
            return i * U + (u + 1)

        def idle_rows(eng, experts):
            for e in experts:
                r = eng.value_load(prow[0:1, e:e + 1], min_val=0, max_val=E * REG - P)
                eng.dma_start(xs[bass.ds(r, P), :], pad).then_inc(s_pd, 16)

        def n2(i, u):
            return i * (U // 2 * 16) + (u // 2 + 1) * 16

        @block.sync
        def _(sp):
            sp.dma_start(bsp[:, 0:NB1 // P], b1.rearrange("e n -> (e n)").rearrange("(p n) -> p n", p=P)).then_inc(s_bl, 16)
            sp.dma_start(bsp[:, NB1 // P:], b2.rearrange("e n -> (e n)").rearrange("(p n) -> p n", p=P)).then_inc(s_bl, 16)
            for e in range(E):
                pieces = []
                for c in range(KC):
                    at = (e * KC + c) * 2 * F
                    for dst, src in ((w1h, w1p[0]), (w1l, w1p[1])):
                        pieces.append((dst[:, at:at + 2 * F].bitcast(F32), src[e * D + c * P:e * D + (c + 1) * P, :]))
                pieces.append((w2s[:, e * FC * D:(e + 1) * FC * D].rearrange("p (c n) -> p c n", c=FC),
                               w2[e].rearrange("(c p) n -> p c n", p=P)))
                for k, (dst, src) in enumerate(pieces):
                    if e > 0:
                        sp.wait_ge(s_we[e if k else e - 1], 16 * (k if k else len(pieces)))
                    sp.dma_start(dst, src).then_inc(s_we[e], 16)
                    if e > 0 and k == 0:
                        sp.sem_inc(s_ready, 1)
                if e == 0:
                    sp.wait_ge(s_pad, 1)
                    idle_rows(sp, range(E // 2, E))
                    sp.dma_start(out[T:T + P, :], pad[:, 0:D]).then_inc(s_pd, 16)
                    sp.wait_ge(s_bs, 5)
                    sp.wait_ge(s_bz, 1)
                    for k in range(3):
                        sp.dma_start(bp[k:k + 1, 0:NB1].rearrange("o (p n) -> o p n", p=P),
                                     bpt[:, k, 0:NB1 // P]).then_inc(s_bd, 16)
                        sp.dma_start(bp[k:k + 1, NB1:].rearrange("o (p n) -> o p n", p=P),
                                     bpt[:, k, NB1 // P:]).then_inc(s_bd, 16)
                    sp.wait_ge(s_ld[1], 16)
            sp.wait_ge(s_we[E - 1], 16 * len(pieces))
            sp.sem_inc(s_ready, 1)

        @block.tensor
        def _(pe):
            mm = nc.tensor.matmul
            mm(bank[0][:, 0:E], ones_bf[:], cm[:, GB, :], start=True, stop=True).then_inc(s_cnt, 1)
            pe.wait_ge(s_bd, 16 * 6)

            def to_T(i, u):
                pe.wait_ge(s_ld[u % 2], n2(i, u))
                if real(i, u - 1):
                    pe.wait_ge(s_xl, n(i, u - 1))
                for c in range(KC):
                    last = nc.tensor.transpose(bank[4][:, c * P:(c + 1) * P], xb[:, u % 2, c * P:(c + 1) * P], ident)
                last.then_inc(s_xT, 1)

            def up(i, u, e, half):
                bk = bank[2 * (u % 2) + half]
                for c in range(KC):
                    h, l = (t[:, u % 2, c * P:(c + 1) * P] for t in (xh, xl))
                    at = e * (KC * 2 * F) + (c * 2 * F + half * F)
                    mm(bk[:, :], h, w1h[:, bass.ds(at, F)], start=(c == 0), stop=False)
                    mm(bk[:, :], h, w1l[:, bass.ds(at, F)], start=False, stop=False)
                    mm(bk[:, :], l, w1h[:, bass.ds(at, F)], start=False, stop=False)
                return mm(bk[:, :], sel3[:], bp[:, bass.ds(e * (2 * F) + half * F, F)], start=False, stop=True)

            def act_T(i, u):
                pe.wait_ge(s_ac, n(i, u))
                if real(i, u - 1):
                    pe.wait_ge(s_aT, n(i, u - 1))
                for c in range(FC):
                    last = nc.tensor.transpose(bank[5][:, c * P:(c + 1) * P], ac[:, c * P:(c + 1) * P], ident)
                last.then_inc(s_at, 1)

            def down(i, u, e):
                pe.wait_ge(s_aT, n(i, u))
                if real(i, u - 2):
                    pe.wait_ge(s_yg, n(i, u - 2))
                bk = bank[6 + u % 2]
                for c in range(FC):
                    mm(bk[:, 0:D], aT[:, c, :], w2s[:, bass.ds(e * (FC * D) + c * D, D)], start=(c == 0), stop=False)
                mm(bk[:, 0:D], sel3[:], bp[:, bass.ds(e * D + NB1, D)], start=False, stop=True).then_inc(s_y, 1)

            def expert(i, u):
                return pe.value_load(tab[0:1, 0, bass.ds(blk(i, u), 1)], min_val=0, max_val=E - 1)

            def slot(i, u):
                if real(i, u - 1):
                    act_T(i, u - 1)
                if real(i, u + 1):
                    to_T(i, u + 1)
                pe.wait_ge(s_xl, n(i, u))
                e = expert(i, u)
                pe.wait_ge(s_ready, e + 1)
                if real(i, u - 2):
                    pe.wait_ge(s_sa, n(i, u - 2))
                up(i, u, e, 0).then_inc(s_a, 1)
                if real(i, u - 2):
                    pe.wait_ge(s_ac, n(i, u - 2))
                up(i, u, e, 1).then_inc(s_g, 1)
                if real(i, u - 1):
                    down(i, u - 1, expert(i, u - 1))

            def last(i):
                act_T(i, -1)
                down(i, -1, expert(i, -1))

            turns(pe, lambda: to_T(0, 0), slot, last)

        @block.scalar
        def _(act):
            def load(i, u):
                r = act.value_load(tab[0:1, 1, bass.ds(blk(i, u), 1)], min_val=0, max_val=E * REG)
                if real(i, u - 2):
                    act.wait_ge(s_xT, n(i, u - 2))
                    act.wait_ge(s_meta, n(i, u - 2))
                act.dma_start(xb[:, u % 2, :], xs[bass.ds(r, P), :]).then_inc(s_ld[u % 2], 16)

            def first():
                act.wait_ge(s_pad, 1)
                idle_rows(act, range(E // 2))
                act.dma_start(xs[E * REG:E * REG + P, :], pad).then_inc(s_pd, 16)
                act.wait_ge(s_pd, 16 * (E + 2))
                load(0, 0)
                load(0, 1)
                x_hi(0, 0)

            def x_hi(i, u):
                act.wait_ge(s_xT, n(i, u))
                if real(i, u - 2):
                    act.wait_ge(s_g, n(i, u - 2))
                nc.scalar.activation(xh[:, u % 2, :], bank[4][:, 0:D], ACT.Copy).then_inc(s_xh, 1)

            def slot(i, u):
                if real(i, u + 2):
                    load(i, u + 2)
                if real(i, u - 1):
                    act.wait_ge(s_at, n(i, u - 1))
                    if real(i, u - 2):
                        act.wait_ge(s_y, n(i, u - 2))
                    nc.scalar.activation(aT[:].rearrange("p c n -> p (c n)"), bank[5][:, :], ACT.Copy).then_inc(s_aT, 1)
                if real(i, u + 1):
                    x_hi(i, u + 1)
                act.wait_ge(s_a, n(i, u))
                if real(i, u - 1):
                    act.wait_ge(s_ac, n(i, u - 1))
                nc.scalar.activation(sa[:], bank[2 * (u % 2)][:, :], ACT.Silu).then_inc(s_sa, 1)

            def last(i):
                act.wait_ge(s_at, n(i, -1))
                act.wait_ge(s_y, n(i, -2))
                nc.scalar.activation(aT[:].rearrange("p c n -> p (c n)"), bank[5][:, :], ACT.Copy).then_inc(s_aT, 1)

            turns(act, first, slot, last)

        @block.vector
        def _(dve):
            V = nc.vector
            V.memset(sel3[:], 0.0).then_inc(s_t, 1)
            V.memset(pad, 0.0).then_inc(s_t, 1)
            dve.wait_ge(s_t, 2)
            V.memset(sel3[0:3, :], 1.0)
            steps = [2]

            def step(ins):
                steps[0] += 1
                ins.then_inc(s_t, 1)
                dve.wait_ge(s_t, steps[0])

            V.tensor_scalar(pad[:, TOK:TOK + 1].bitcast(I32), consts[:, C_P:C_P + 1], float(T), None, ALU.add)
            dve.wait_ge(s_cnt, 1)
            step(V.tensor_copy(cnt[:], bank[0][:, 0:E]))
            scr = scratch[:, 0:E * NTH].rearrange("p (e k) -> p e k", e=E)
            step(V.tensor_tensor(scr, cnt[:].rearrange("p (e o) -> p e o", o=1).to_broadcast([P, E, NTH]),
                                 consts[:, C_THR:C_THR + NTH].rearrange("p (o k) -> p o k", o=1).to_broadcast([P, E, NTH]),
                                 ALU.is_gt))
            step(V.tensor_reduce(nbk[:], scr, AX_X, ALU.add))
            scr = scratch[:, 0:E * E].rearrange("p (e k) -> p e k", e=E)
            step(V.tensor_tensor(scr, consts[:, C_T8:C_T8 + E * E].rearrange("p (e k) -> p e k", e=E),
                                 nbk[:].rearrange("p (o k) -> p o k", o=1).to_broadcast([P, E, E]), ALU.mult))
            step(V.tensor_reduce(incl[:], scr, AX_X, ALU.add))
            scr = flat[:, 0:NT * E].rearrange("p (b e) -> p b e", e=E)
            step(V.tensor_tensor(scr, consts[0:1, C_BLK:C_BLK + NT].rearrange("p (b o) -> p b o", o=1).to_broadcast([1, NT, E]),
                                 incl[0:1, :].rearrange("p (o e) -> p o e", o=1).to_broadcast([1, NT, E]), ALU.is_ge))
            step(V.tensor_reduce(ej, scr, AX_X, ALU.add))
            step(V.tensor_tensor(scr, scr, nbk[0:1, :].rearrange("p (o e) -> p o e", o=1).to_broadcast([1, NT, E]), ALU.mult))
            step(V.tensor_reduce(st, scr, AX_X, ALU.add))
            step(V.tensor_tensor(st, consts[0:1, C_BLK:C_BLK + NT], st, ALU.subtract))
            step(V.tensor_scalar(st, st, float(P), None, ALU.mult))
            step(V.scalar_tensor_tensor(st, ej, float(REG), st, ALU.mult, ALU.add))
            step(V.tensor_scalar(tab[:, 1, :], st, float(E * REG), None, ALU.min))
            step(V.tensor_scalar(tab[:, 0, :], ej, float(E - 1), None, ALU.min))
            step(V.tensor_tensor(prf[:], cnt[0:1, :], consts[0:1, C_BASE:C_BASE + E], ALU.add))
            V.tensor_copy(prow[:], prf[:]).then_inc(s_tab, 1)
            dve.wait_ge(s_tab, 1)
            dve.sem_inc(s_pad, 1)
            dve.wait_ge(s_bl, 32)
            bsteps = [0]

            def bstep(ins):
                bsteps[0] += 1
                ins.then_inc(s_bs, 1)
                dve.wait_ge(s_bs, bsteps[0])

            bstep(V.tensor_copy(bpt[:, 0, :], bsp[:]))
            bstep(V.tensor_tensor(bsp[:], bsp[:], bpt[:, 0, :], ALU.subtract))
            bstep(V.tensor_copy(bpt[:, 1, :], bsp[:]))
            bstep(V.tensor_tensor(bsp[:], bsp[:], bpt[:, 1, :], ALU.subtract))
            bstep(V.tensor_copy(bpt[:, 2, :], bsp[:]))

            def x_lo(i, u):
                dve.wait_ge(s_xh, n(i, u))
                V.tensor_tensor(xl[:, u % 2, :], bank[4][:, 0:D], xh[:, u % 2, :].bitcast(F32), ALU.subtract).then_inc(s_xl, 1)
                if real(i, u - U):
                    dve.wait_ge(s_add, i * (U * 16) + (u - U + 1) * 16)
                V.tensor_copy(tk[:, u % U:u % U + 1], xb[:, u % 2, TOK:TOK + 1].bitcast(I32))
                e = dve.value_load(tab[0:1, 0, bass.ds(blk(i, u), 1)], min_val=0, max_val=E - 1)
                V.tensor_copy(gt[:, u % U:u % U + 1], xb[:, u % 2, bass.ds(e + GATE, 1)]).then_inc(s_meta, 1)

            def gate(i, u):
                dve.wait_ge(s_y, n(i, u))
                dve.wait_ge(s_meta, n(i, u))
                if real(i, u - 2):
                    dve.wait_ge(s_add, i * (U * 16) + (u - 2 + 1) * 16)
                V.tensor_scalar(yg[:, u % 2, :], bank[6 + u % 2][:, 0:D], gt[:, u % U:u % U + 1], None, ALU.mult).then_inc(s_yg, 1)

            def slot(i, u):
                if real(i, u + 1):
                    x_lo(i, u + 1)
                dve.wait_ge(s_g, n(i, u))
                dve.wait_ge(s_sa, n(i, u))
                if real(i, u - 1):
                    dve.wait_ge(s_at, n(i, u - 1))
                V.tensor_tensor(ac[:], bank[2 * (u % 2) + 1][:, :], sa[:], ALU.mult).then_inc(s_ac, 1)
                if real(i, u - 1):
                    gate(i, u - 1)

            turns(dve, lambda: x_lo(0, 0), slot, lambda i: gate(i, -1))

        @block.gpsimd
        def _(pool):
            nc.gpsimd.memset(bp[:].bitcast(U32), 0).then_inc(s_bz, 1)

            def slot(i, u):
                pool.wait_ge(s_yg, n(i, u))
                if real(i, u - 1):
                    pool.wait_ge(s_add, i * (U * 16) + u * 16)
                pool.sem_inc(s_turn, 1)
                nc.gpsimd.indirect_dma_start(out=out[:, :],
                                             out_offset=bass.IndirectOffsetOnAxis(ap=tk[:, u:u + 1], axis=0),
                                             in_=yg[:, u % 2, :], in_offset=None, compute_op=ALU.add).then_inc(s_add, 16)

            turns(pool, lambda: None, slot, lambda i: None)
            pool.wait_ge(s_add, 16 * NT)


_INS = ["x", "ctx_1024", "L0_xattn_W_q", "L0_xattn_W_k", "L0_xattn_W_v", "L0_xattn_W_out", "L0_xattn_b_q", "L0_xattn_b_k",
        "L0_xattn_b_v", "L0_xattn_b_out", "L0_ffn_W1", "L0_ffn_b1", "L0_ffn_W2", "L0_ffn_b2", "L0_ffn_Wr", "L0_ffn_br"]
_TRANSPOSED = ("L0_xattn_W_q", "L0_xattn_W_k", "L0_xattn_W_v", "L0_xattn_W_out")


def shape_constants(NB):
    import numpy as np
    T, REG, NBLK = sizes(NB)
    c = np.zeros((P, C_END), np.float32)
    r = np.arange(P)
    c[:, C_ID:C_ID + P] = np.eye(P)
    c[:, C_TRI:C_TRI + P] = r[:, None] < r[None, :]
    c[:, C_ONE:C_ONE + P] = 1
    c[:, C_I8:C_I8 + E] = np.arange(E)
    c[:, C_BASE:C_BASE + E] = np.arange(E) * REG
    c[:, C_THR:C_THR + NB] = np.arange(NB) * P
    c[:, C_BLK:C_BLK + 144] = np.arange(144)
    e = np.arange(E)
    c[:, C_T8:C_T8 + E * E] = (e[None, :] <= e[:, None]).reshape(-1)
    c[:, C_P] = r
    return c


def kernel(**inputs):
    import numpy as _np
    import concourse.bacc as _bacc
    from concourse.bass_utils import run_bass_kernel_spmd as _run

    nc = _bacc.Bacc("TRN2", target_bir_lowering=False, num_devices=1)
    arrays, args = {}, []
    NB = inputs["x"].shape[0]
    laid = {n: _np.ascontiguousarray(_np.asarray(inputs[n]).T if n in _TRANSPOSED else inputs[n]) for n in _INS}
    laid["constants"] = shape_constants(NB)
    for name, a in laid.items():
        arrays[f"in_{name}"] = a
        args.append(nc.dram_tensor(f"in_{name}", a.shape, mybir.dt.from_np(a.dtype), kind="ExternalInput").ap())
    args.append(nc.dram_tensor("out_rows", (NB * P + P, D), F32, kind="ExternalOutput").ap())
    moe_layer(nc, *args)
    r = _run(nc, [arrays], core_ids=[0])
    return r.results[0]["out_rows"][:NB * P].reshape(NB, P, D)
```
